# Optimizing a Trainium2 kernel written in Bass

```python
import numpy as np
import jax
import jax.numpy as jnp

def _softmax(x, axis=-1):
    return jax.nn.softmax(x, axis=axis)

def _gelu(x):
    return jax.nn.gelu(x, approximate=True)

def _silu(x):
    return jax.nn.silu(x)

def _sigmoid(x):
    return jax.nn.sigmoid(x)

def _layernorm(x, axis=-1, eps=1e-05):
    m = jnp.mean(x, axis=axis, keepdims=True)
    v = jnp.var(x, axis=axis, keepdims=True)
    return (x - m) / jnp.sqrt(v + eps)

def _scatter_add(tgt, idx, src, axis=0):
    return tgt.at[idx].add(src)

def _segment_sum(src, seg, n):
    return jax.ops.segment_sum(src, seg, n)
kernel_name = 'mk_cond_resid_d4_seqx_r4_1d0675'

def setup_inputs(seed: int=0):
    np.random.seed(seed)
    _w = jnp.asarray

    def _rec_inputs():
        import jax
        import jax.numpy as jnp
        _rk = jax.random.key(seed)
        x = -0.000125 + 0.9999 * jax.random.normal(jax.random.fold_in(_rk, 1), (32, 256, 256), jnp.float32)
        _lenS = 256 - jax.random.randint(jax.random.fold_in(_rk, 7), (32,), 0, max(1, 256 // 4) + 1, jnp.int32)
        _lenS2 = 256 - jax.random.randint(jax.random.fold_in(_rk, 8), (32,), 0, max(1, 256 // 4) + 1, jnp.int32)
        cond_512 = 0.0061147 + 1.02565 * jax.random.normal(jax.random.fold_in(_rk, 11), (32, 128), jnp.float32)
        return (x, cond_512)
    x, cond_512 = _rec_inputs()

    def _L0_cond_setup():
        import jax, jax.numpy as jnp
        import numpy as np
        B, S, D, H, C = (8, 1024, 256, 64, 128)
        INIT_RANGE = 0.01
        key = jax.random.key(seed)
        ks = jax.random.split(key, 6)
        return {'hidden_states': jax.random.normal(ks[0], (B, S, D), dtype=jnp.float32), 'conditions': jax.random.normal(ks[1], (B, C), dtype=jnp.float32), 'down_project': jax.random.normal(ks[2], (D, H), dtype=jnp.float32) * INIT_RANGE, 'down_gamma': jax.random.normal(ks[3], (C, H), dtype=jnp.float32), 'down_beta': jnp.zeros((C, H), dtype=jnp.float32), 'up_project': jax.random.normal(ks[4], (H, D), dtype=jnp.float32) * INIT_RANGE, 'up_gamma': jax.random.normal(ks[5], (C, D), dtype=jnp.float32), 'up_beta': jnp.zeros((C, D), dtype=jnp.float32)}
    _L0_cond_all = _L0_cond_setup()
    _L0_cond_in = {k: v for k, v in _L0_cond_all.items() if k in ('down_project', 'down_gamma', 'down_beta', 'up_project', 'up_gamma', 'up_beta')}
    del _L0_cond_all

    def _L1_cond_setup():
        import jax, jax.numpy as jnp
        import numpy as np
        W_DIM = 128
        CLAMP = 256.0
        key = jax.random.key(seed)
        ks = jax.random.split(key, 6)
        B, L, C = (8, 2048, 256)
        return {'x': jax.random.normal(ks[0], (B, L, C), dtype=jnp.float32), 'w': jax.random.normal(ks[1], (B, W_DIM), dtype=jnp.float32), 'weight': jax.random.normal(ks[2], (C, C), dtype=jnp.float32), 'bias': jax.random.normal(ks[3], (C,), dtype=jnp.float32), 'affine_w': jax.random.normal(ks[4], (C, W_DIM), dtype=jnp.float32), 'affine_b': jnp.ones((C,), dtype=jnp.float32)}
    _L1_cond_all = _L1_cond_setup()
    _L1_cond_in = {k: v for k, v in _L1_cond_all.items() if k in ('weight', 'bias', 'affine_w', 'affine_b')}
    del _L1_cond_all

    def _L2_cond_setup():
        import jax, jax.numpy as jnp
        import numpy as np
        import math
        HEAD_NUM = 16
        EPS = 1e-08

        def modulated_linear(x, s, aff_w, aff_b, w, b):
            style = s @ aff_w.T + aff_b
            w_mod = w[None, :, :] * style[:, None, :]
            demod = jax.lax.rsqrt(jnp.sum(w_mod * w_mod, axis=2) + EPS)
            w_mod = w_mod * demod[:, :, None]
            return jnp.einsum('bni,boi->bno', x, w_mod) + b
        key = jax.random.key(seed)
        ks = jax.random.split(key, 6)
        B, N, F, S = (8, 256, 256, 128)
        return {'x': jax.random.normal(ks[0], (B, N, F), dtype=jnp.float32), 's': jax.random.normal(ks[1], (B, S), dtype=jnp.float32), 'k_aff_w': jax.random.normal(ks[2], (F, S), dtype=jnp.float32) * 0.02, 'k_aff_b': jnp.ones((F,), dtype=jnp.float32), 'k_w': jax.random.normal(ks[3], (F, F), dtype=jnp.float32) * 0.02, 'k_b': jnp.zeros((F,), dtype=jnp.float32), 'o_aff_w': jax.random.normal(ks[4], (F, S), dtype=jnp.float32) * 0.02, 'o_aff_b': jnp.ones((F,), dtype=jnp.float32), 'o_w': jax.random.normal(ks[5], (F, F), dtype=jnp.float32) * 0.02, 'o_b': jnp.zeros((F,), dtype=jnp.float32)}
    _L2_cond_all = _L2_cond_setup()
    _L2_cond_in = {k: v for k, v in _L2_cond_all.items() if k in ('k_aff_w', 'k_aff_b', 'k_w', 'k_b', 'o_aff_w', 'o_aff_b', 'o_w', 'o_b')}
    del _L2_cond_all

    def _L3_cond_setup():
        import jax, jax.numpy as jnp
        import numpy as np
        IN_DIM = 256
        OUT_DIM = 256
        MU_DIM = 128
        K = 30
        key = jax.random.key(seed)
        k1, k2, k3, k4, k5 = jax.random.split(key, 5)
        B, S = (16, 512)
        x = jax.random.normal(k1, (B, S, IN_DIM), dtype=jnp.float32)
        mu = jax.random.normal(k2, (B, MU_DIM), dtype=jnp.float32)
        W_dec = jax.random.normal(k3, (MU_DIM, (IN_DIM + 1) * K), dtype=jnp.float32) / np.sqrt(MU_DIM)
        b_dec = jax.random.normal(k4, ((IN_DIM + 1) * K,), dtype=jnp.float32) * 0.01
        V = jax.random.normal(k5, (K, OUT_DIM), dtype=jnp.float32) / np.sqrt(K)
        return {'x': x, 'mu': mu, 'W_dec': W_dec, 'b_dec': b_dec, 'V': V}
    _L3_cond_all = _L3_cond_setup()
    _L3_cond_in = {k: v for k, v in _L3_cond_all.items() if k in ('W_dec', 'b_dec', 'V')}
    del _L3_cond_all
    return {'x': x, 'cond_512': cond_512, 'L0_cond_down_project': _L0_cond_in['down_project'], 'L0_cond_down_gamma': _L0_cond_in['down_gamma'], 'L0_cond_down_beta': _L0_cond_in['down_beta'], 'L0_cond_up_project': _L0_cond_in['up_project'], 'L0_cond_up_gamma': _L0_cond_in['up_gamma'], 'L0_cond_up_beta': _L0_cond_in['up_beta'], 'L1_cond_weight': _L1_cond_in['weight'], 'L1_cond_bias': _L1_cond_in['bias'], 'L1_cond_affine_w': _L1_cond_in['affine_w'], 'L1_cond_affine_b': _L1_cond_in['affine_b'], 'L2_cond_k_aff_w': _L2_cond_in['k_aff_w'], 'L2_cond_k_aff_b': _L2_cond_in['k_aff_b'], 'L2_cond_k_w': _L2_cond_in['k_w'], 'L2_cond_k_b': _L2_cond_in['k_b'], 'L2_cond_o_aff_w': _L2_cond_in['o_aff_w'], 'L2_cond_o_aff_b': _L2_cond_in['o_aff_b'], 'L2_cond_o_w': _L2_cond_in['o_w'], 'L2_cond_o_b': _L2_cond_in['o_b'], 'L3_cond_W_dec': _L3_cond_in['W_dec'], 'L3_cond_b_dec': _L3_cond_in['b_dec'], 'L3_cond_V': _L3_cond_in['V']}

def reference(x, cond_512, L0_cond_down_project, L0_cond_down_gamma, L0_cond_down_beta, L0_cond_up_project, L0_cond_up_gamma, L0_cond_up_beta, L1_cond_weight, L1_cond_bias, L1_cond_affine_w, L1_cond_affine_b, L2_cond_k_aff_w, L2_cond_k_aff_b, L2_cond_k_w, L2_cond_k_b, L2_cond_o_aff_w, L2_cond_o_aff_b, L2_cond_o_w, L2_cond_o_b, L3_cond_W_dec, L3_cond_b_dec, L3_cond_V):
    import jax
    import jax.numpy as jnp

    def _L0_cond_ref(hidden_states, conditions, down_project, down_gamma, down_beta, up_project, up_gamma, up_beta):
        import jax, jax.numpy as jnp
        import numpy as np
        B, S, D, H, C = (8, 1024, 256, 64, 128)
        INIT_RANGE = 0.01
        dg = conditions @ down_gamma
        db = conditions @ down_beta
        ug = conditions @ up_gamma
        ub = conditions @ up_beta
        w_down = down_project[None, :, :] * dg[:, None, :] + db[:, None, :]
        down = jnp.einsum('bsd,bdh->bsh', hidden_states, w_down)
        act = jax.nn.relu(down)
        w_up = up_project[None, :, :] * ug[:, None, :] + ub[:, None, :]
        up = jnp.einsum('bsh,bhd->bsd', act, w_up)
        return up + hidden_states

    def _L1_cond_ref(x, w, weight, bias, affine_w, affine_b):
        import jax, jax.numpy as jnp
        import numpy as np
        W_DIM = 128
        CLAMP = 256.0
        B, L, C = x.shape
        gain = 1.0 / np.sqrt(W_DIM).astype(np.float32)
        styles = w @ (affine_w * gain).T + affine_b
        ws = weight[None, :, :] * styles[:, None, :]
        dcoefs = jax.lax.rsqrt(jnp.sum(ws * ws, axis=2) + 1e-08)
        xm = x * styles[:, None, :]
        y = jnp.einsum('blc,oc->blo', xm, weight)
        y = y * dcoefs[:, None, :]
        y = jnp.clip(y + bias, -CLAMP, CLAMP)
        return y

    def _L2_cond_ref(x, s, k_aff_w, k_aff_b, k_w, k_b, o_aff_w, o_aff_b, o_w, o_b):
        import jax, jax.numpy as jnp
        import numpy as np
        import math
        HEAD_NUM = 16
        EPS = 1e-08

        def modulated_linear(x, s, aff_w, aff_b, w, b):
            style = s @ aff_w.T + aff_b
            w_mod = w[None, :, :] * style[:, None, :]
            demod = jax.lax.rsqrt(jnp.sum(w_mod * w_mod, axis=2) + EPS)
            w_mod = w_mod * demod[:, :, None]
            return jnp.einsum('bni,boi->bno', x, w_mod) + b
        B, N, F = x.shape
        H = HEAD_NUM
        D = F // H
        kx = modulated_linear(x, s, k_aff_w, k_aff_b, k_w, k_b)
        kx = kx.reshape(B, N, H, D)
        q = k = v = kx
        scores = jnp.einsum('bnhd,bnjd->bnhj', q, k) / math.sqrt(D)
        A = jax.nn.softmax(scores, axis=-1)
        out = jnp.einsum('bnhj,bnjd->bnhd', A, v).reshape(B, N, F)
        out = modulated_linear(out, s, o_aff_w, o_aff_b, o_w, o_b)
        return out

    def _L3_cond_ref(x, mu, W_dec, b_dec, V):
        import jax, jax.numpy as jnp
        import numpy as np
        IN_DIM = 256
        OUT_DIM = 256
        MU_DIM = 128
        K = 30
        B = mu.shape[0]
        U = (mu @ W_dec + b_dec).reshape(B, IN_DIM + 1, K)
        param = jnp.einsum('bik,kj->bij', U, V)
        weight = param[:, :-1, :]
        bias = param[:, -1, :]
        out = jnp.einsum('bsd,bde->bse', x, weight)
        out = out + bias[:, None, :]
        return out
    x = x + _L0_cond_ref(x, cond_512, L0_cond_down_project, L0_cond_down_gamma, L0_cond_down_beta, L0_cond_up_project, L0_cond_up_gamma, L0_cond_up_beta)
    x = x + _L1_cond_ref(x, cond_512, L1_cond_weight, L1_cond_bias, L1_cond_affine_w, L1_cond_affine_b)
    x = x + _L2_cond_ref(x, cond_512, L2_cond_k_aff_w, L2_cond_k_aff_b, L2_cond_k_w, L2_cond_k_b, L2_cond_o_aff_w, L2_cond_o_aff_b, L2_cond_o_w, L2_cond_o_b)
    x = x + _L3_cond_ref(x, cond_512, L3_cond_W_dec, L3_cond_b_dec, L3_cond_V)
    return x

_drawn_inputs = setup_inputs


def setup_inputs(seed=0):
    import zlib

    import numpy as np

    out = dict(_drawn_inputs(seed))
    spreads = {'L0_cond_down_beta': (0.0, 0.1),
     'L0_cond_up_beta': (0.0, 0.1),
     'L1_cond_affine_b': (1.0, 0.2),
     'L2_cond_k_aff_b': (1.0, 0.2),
     'L2_cond_k_b': (0.0, 2.0),
     'L2_cond_o_aff_b': (1.0, 0.2),
     'L2_cond_o_b': (0.0, 2.0)}
    factors = {'L1_cond_bias': 43.657, 'L3_cond_b_dec': 6.201}
    for name, (base, spread) in spreads.items():
        noise = np.random.default_rng([zlib.crc32(name.encode()), seed]).standard_normal(out[name].shape)
        drawn = base * np.exp(spread * noise) if base else spread * noise
        out[name] = jnp.asarray(drawn.astype(out[name].dtype))
    for name, factor in factors.items():
        out[name] = (out[name] * factor).astype(out[name].dtype)
    return out
```

```python
from contextlib import ExitStack

import numpy as np

import concourse.bass as bass
from concourse import mybir

F32 = mybir.dt.float32
BF16 = mybir.dt.bfloat16
ALU = mybir.AluOpType
ACT = mybir.ActivationFunctionType
AX = mybir.AxisListType

P = 128
C = 2
H, DH = 16, 16
G = 8
NU = 32
CLAMP = 256.0
EPS = 1e-8
PARTS = 3
PAIRS = [(0, 0), (0, 1), (0, 2), (1, 0), (1, 1), (2, 0)]

PA_STYLE1, PA_STYLEK, PA_DEMOD1, PA_N = 0, 2, 4, 6
PB_STYLEO, PB_DEMODO, PB_ULAST, PB_U = 0, 2, 4, 5


def build(nc, xT, condT, gb_down, gb_up, dproj, uproj, w1T, bias1, aff1T, affb1, wkT, affkT, affbk, kb,
          woT, affoT, affbo, ob, wdec, bdec, bdec_last, vmat, ident, outT):
    B, _, _, S = xT.shape
    D = C * P
    HID = uproj.shape[0]
    K = vmat.shape[0]
    CD = condT.shape[0]
    GAIN = float(np.float32(1.0) / np.sqrt(CD).astype(np.float32))
    SCALE = 1.0 / float(np.sqrt(DH))
    PB_N = PB_U + C * K
    NROW = 2 * HID + 2 * D + D
    R_DG, R_DB, R_UG, R_UB, R_DK = 0, HID, 2 * HID, 2 * HID + D, 2 * HID + 2 * D
    W = C * S
    assert W == 512 and S == 2 * P and D == H * DH

    with ExitStack() as ctx:
        def sb(name, shape, dt=F32):
            return ctx.enter_context(nc.sbuf_tensor(name, shape, dt))

        def psum(name):
            return ctx.enter_context(nc.psum_tensor(name, [P, W], F32))

        def sem(name):
            return ctx.enter_context(nc.semaphore(name))

        rows_dram = nc.dram_tensor("rows_dram", [B, NROW], F32).ap()

        cond = sb("cond", [CD, B])
        gbd, gbu = sb("gbd", [CD, 2 * HID]), sb("gbu", [CD, 2 * D])
        dpj, upj = sb("dpj", [P, C, HID]), sb("upj", [HID, D])
        w1s, wks, wos = sb("w1s", [P, C, D]), sb("wks", [P, C, D]), sb("wos", [P, C, D])
        afs = [sb(f"aff{n}", [CD, D]) for n in range(3)]
        afb = sb("afb", [P, 3, C])
        b1s, obs = sb("b1s", [P, C]), sb("obs", [P, C])
        kbs = sb("kbs", [P, D])
        bds, bdl = sb("bds", [P, C, K]), sb("bdl", [K, 1])
        vms = sb("vms", [K, D])
        idn = sb("idn", [P, P])
        rows = sb("rows", [B, NROW])
        pa_all, pb_all = sb("pa_all", [P, B, PA_N]), sb("pb_all", [P, B, PB_N])
        sty = sb("sty", [P, 3, C, B])
        sty2 = sb("sty2", [P, 3, C, B])
        dem = sb("dem", [P, 2, C, B])
        dt1, dt2 = sb("dt1", [P, 2, C, B]), sb("dt2", [P, 2, C, B])
        rk0, rk1 = sb("rk0", [B, D]), sb("rk1", [B, D])
        bc = sb("bc", [P, 2, NROW])
        pa, pb = sb("pa", [P, PA_N]), sb("pb", [P, PB_N])
        wd, wu = sb("wd", [P, C, HID]), sb("wu", [HID, D])
        w1, wk, wo = sb("w1", [P, C, D]), sb("wk", [P, C, D]), sb("wo", [P, C, D])
        xin = sb("xin", [P, 2, W])
        hid = sb("hid", [HID, S])
        x1, y1, yc = sb("x1", [P, W]), sb("y1", [P, W]), sb("yc", [P, W])
        x2 = sb("x2", [P, 2, W])
        kx = sb("kx", [P, W])
        k3, v3, a3 = sb("k3", [P, PARTS, W]), sb("v3", [P, PARTS, W]), sb("a3", [P, PARTS, W])
        bk, bv = sb("bk", [P, PARTS * G * W]), sb("bv", [P, PARTS * G * W])
        smax, ssum, sinv = sb("smax", [P, NU]), sb("ssum", [P, NU]), sb("sinv", [P, NU])
        sd, ex, pr = sb("sd", [P, W]), sb("ex", [P, W]), sb("pr", [P, W])
        on, ot = sb("on", [P, W]), sb("ot", [P, W])
        zz, x3 = sb("zz", [P, W]), sb("x3", [P, W])
        rr = sb("rr", [K, S])
        xo = sb("xo", [P, 2, W])
        wds = bv[:, 0:(D + 1) * K]

        ps_h, ps_f, ps_1, ps_k, ps_s, ps_a, ps_t, ps_o = (
            psum(n) for n in ("ps_h", "ps_f", "ps_1", "ps_k", "ps_s", "ps_a", "ps_t", "ps_o"))

        ld_small = sem("ld_small")
        ld_wdec = sem("ld_wdec")
        rows_out = sem("rows_out")
        x_in = [sem("x_in0"), sem("x_in1")]
        bc_in = [sem("bc_in0"), sem("bc_in1")]
        out_st = [sem("out_st0"), sem("out_st1")]
        bk_in, bv_in = sem("bk_in"), sem("bv_in")
        zero_k, zero_v = sem("zero_k"), sem("zero_v")
        su_pe, su_act, su_dve = sem("su_pe"), sem("su_act"), sem("su_dve")
        pa_ready, pb_ready, w1_ready, wo_ready = sem("pa_ready"), sem("pb_ready"), sem("w1_ready"), sem("wo_ready")
        wd_half, wu_half = sem("wd_half"), sem("wu_half")
        wd_ready, wu_ready, wk_ready = sem("wd_ready"), sem("wu_ready"), sem("wk_ready")
        down_done, up_done, l1_done, key_done = sem("down_done"), sem("up_done"), sem("l1_done"), sem("key_done")
        hid_ready, x1_ready, y1_ready, yc_ready, x2_ready = (
            sem("hid_ready"), sem("x1_ready"), sem("y1_ready"), sem("yc_ready"), sem("x2_ready"))
        kx_ready, k0_ready, k1_ready, k3_ready = sem("kx_ready"), sem("k0_ready"), sem("k1_ready"), sem("k3_ready")
        v0_ready, v1_ready, v3_ready = sem("v0_ready"), sem("v1_ready"), sem("v3_ready")
        s_done, max_ready, sd_ready, ex_ready = sem("s_done"), sem("max_ready"), sem("sd_ready"), sem("ex_ready")
        sum_ready, inv_ready, pr_ready = sem("sum_ready"), sem("inv_ready"), sem("pr_ready")
        a0_ready, a1_ready, a3_ready = sem("a0_ready"), sem("a1_ready"), sem("a3_ready")
        av_done, on_ready, t_done, ot_ready = sem("av_done"), sem("on_ready"), sem("t_done"), sem("ot_ready")
        o_done, z_ready, x3_ready = sem("o_done"), sem("z_ready"), sem("x3_ready")
        r_done, rr_ready, l3_done, xo_ready = sem("r_done"), sem("rr_ready"), sem("l3_done"), sem("xo_ready")

        def after(eng, s, b, per=1):
            if isinstance(b, int) and b < 0:
                return
            eng.wait_ge(s, (b + 1) * per if per > 1 else b + 1)

        def pair_count(b, par):
            return (b - par) * 8 + 16

        def halves(t):
            return t.bitcast(BF16)

        N_SMALL = 21
        SU_STY, SU_STY2, SU_VAR, SU_ROWS, SU_U = 3, 5, 6, 11, 18
        LOOPED = B - 2

        def steps(eng, step):
            step(-2, 0, do_p=True)
            step(-1, 1, do_p=True, do_s=True)
            step(0, 0, do_p=True, do_s=True, do_q=True)
            step(1, 1, do_p=True, do_s=True, do_q=True)
            with eng.Fori(2, LOOPED - 1, 2) as i:
                step(i, 0, do_p=True, do_s=True, do_q=True)
                step(i + 1, 1, do_p=True, do_s=True, do_q=True)
            step(B - 2, 0, do_s=True, do_q=True)
            step(B - 1, 1, do_q=True)

        block = ctx.enter_context(nc.Block())

        @block.sync
        def _(sp):
            small = [(cond[:, :], condT), (afs[0][:, :], aff1T), (afs[1][:, :], affkT), (afs[2][:, :], affoT),
                     (afb[:, 0, :], affb1), (afb[:, 1, :], affbk), (afb[:, 2, :], affbo),
                     (w1s[:, :, :], w1T), (wks[:, :, :], wkT), (wos[:, :, :], woT),
                     (gbd[:, :], gb_down), (gbu[:, :], gb_up),
                     (dpj[:, :, :], dproj), (upj[:, :], uproj), (b1s[:, :], bias1), (obs[:, :], ob),
                     (kbs[:, :], kb.to_broadcast([P, D])), (bds[:, :, :], bdec), (bdl[:, :], bdec_last),
                     (vms[:, :], vmat), (idn[:, :], ident)]
            assert len(small) == N_SMALL
            for dst, src in small:
                sp.dma_start(dst, src).then_inc(ld_small, 16)
            sp.dma_start(wds, wdec).then_inc(ld_wdec, 16)
            sp.dma_start(xin[:, 0, :], xT[0].rearrange("p c s -> p (c s)")).then_inc(x_in[0], 16)
            sp.dma_start(xin[:, 1, :], xT[1].rearrange("p c s -> p (c s)")).then_inc(x_in[1], 16)
            sp.wait_ge(su_dve, SU_ROWS)
            sp.dma_start(rows_dram, rows[:, :]).then_inc(rows_out, 16)
            sp.wait_ge(rows_out, 16)
            for b in range(2):
                sp.dma_start(bc[:, b, :], rows_dram[b:b + 1, :].to_broadcast([P, NROW])).then_inc(bc_in[b], 16)

            def keys_to_diagonal(b):
                after(sp, k3_ready, b)
                after(sp, s_done, b - 1)
                dst = bk[:, :].rearrange("p (w t n) -> p w t n", w=PARTS, t=G)
                for t in range(G):
                    sp.dma_start(dst[16 * t:16 * t + 16, :, t, :], k3[16 * t:16 * t + 16, :, :]).then_inc(bk_in, 16)

            def values_to_diagonal(b):
                after(sp, v3_ready, b)
                after(sp, av_done, b - 1)
                dst = bv[:, :].rearrange("p (w a t n) -> p w a t n", w=PARTS, a=2, t=G)
                src = v3[:, :, :].rearrange("p w (v n) -> p w v n", v=2)
                for q in range(4):
                    for v in range(2):
                        for a in range(2):
                            to, at = 32 * q + 16 * v, 32 * q + 16 * a
                            sp.dma_start(dst[to:to + 16, :, a, 2 * q + v, :], src[at:at + 16, :, v, :]).then_inc(bv_in, 16)

            def to_diagonal(b):
                keys_to_diagonal(b)
                values_to_diagonal(b)

            sp.wait_ge(zero_k, 1)
            sp.wait_ge(zero_v, 1)
            to_diagonal(0)
            with sp.Fori(1, B - 1, 2) as b:
                to_diagonal(b)
                to_diagonal(b + 1)
            to_diagonal(B - 1)


        @block.tensor
        def _(pe):
            pe.wait_ge(ld_small, 16 * N_SMALL)
            for n in range(3):
                for c in range(C):
                    mm = pe.matmul(ps_h[:, (n * C + c) * B:(n * C + c + 1) * B], afs[n][:, c * P:(c + 1) * P],
                                   cond[:, :], start=True, stop=True, skip_group_check=True)
            mm.then_inc(su_pe, 1)
            pe.matmul(ps_f[0:B, 0:2 * HID], cond[:, :], gbd[:, :], start=True, stop=True)
            pe.matmul(ps_1[0:B, :], cond[:, :], gbu[:, :], start=True, stop=True).then_inc(su_pe, 1)
            pe.wait_ge(su_act, 1)
            pe.wait_ge(su_dve, SU_STY2)
            for n, sq in ((0, x2[:, 0, :]), (1, x2[:, 1, :])):
                for o in range(C):
                    for c in range(C):
                        mm = pe.matmul(ps_k[:, (n * C + o) * B:(n * C + o + 1) * B],
                                       sq[:, c * D + o * P:c * D + (o + 1) * P], sty2[:, 2 * n, c, :],
                                       start=(c == 0), stop=(c == C - 1), skip_group_check=True)
            for c in range(C):
                mm = pe.matmul(ps_s[0:B, 0:D], sty2[:, 1, c, :], x3[:, c * D:(c + 1) * D],
                               start=(c == 0), stop=(c == C - 1))
            mm.then_inc(su_pe, 1)
            pe.wait_ge(ld_wdec, 16)
            banks = (ps_a, ps_t, ps_o, ps_h)
            for c in range(C):
                for k in range(K):
                    bank, at = banks[2 * c + k // 16], (k % 16) * B
                    mm = pe.matmul(bank[:, at:at + B], wds[:, c * P * K + k:c * P * K + k + (P - 1) * K + 1:K],
                                   cond[:, :], start=True, stop=True, skip_group_check=True)
            mm.then_inc(su_pe, 1)
            pe.wait_ge(su_dve, SU_VAR)
            pe.matmul(ps_k[0:K, 0:B], wds[:, D * K:(D + 1) * K], cond[:, :], start=True, stop=True).then_inc(su_pe, 1)
            pe.wait_ge(su_dve, SU_U)

            def down(b, par):
                after(pe, wd_ready, b)
                pe.wait_ge(x_in[par], pair_count(b, par))
                after(pe, hid_ready, b - 1)
                after(pe, rr_ready, b - 3)
                for c in range(C):
                    mm = pe.matmul(ps_h[0:HID, 0:S], wd[:, c, :], xin[:, par, c * S:(c + 1) * S],
                                   start=(c == 0), stop=(c == C - 1))
                mm.then_inc(down_done, 1)

            def up(b):
                after(pe, wu_ready, b)
                after(pe, hid_ready, b)
                after(pe, x1_ready, b - 1)
                after(pe, xo_ready, b - 3)
                for c in range(C):
                    mm = pe.matmul(ps_f[:, c * S:(c + 1) * S], wu[:, c * P:(c + 1) * P], hid[:, :],
                                   start=True, stop=True, skip_group_check=True)
                mm.then_inc(up_done, 1)

            def l1(b):
                after(pe, w1_ready, b)
                after(pe, x1_ready, b)
                after(pe, y1_ready, b - 1)
                for o in range(C):
                    for c in range(C):
                        mm = pe.matmul(ps_1[:, o * S:(o + 1) * S], w1[:, c, o * P:(o + 1) * P],
                                       x1[:, c * S:(c + 1) * S], start=(c == 0), stop=(c == C - 1),
                                       skip_group_check=True)
                mm.then_inc(l1_done, 1)

            def key(b, par):
                after(pe, wk_ready, b)
                after(pe, x2_ready, b)
                after(pe, kx_ready, b - 1)
                for a in range(2):
                    for c in range(C):
                        mm = pe.matmul(ps_k[:, a * D:(a + 1) * D], x2[:, par, c * S + a * P:c * S + (a + 1) * P],
                                       wk[:, c, :], start=(c == 0), stop=(c == C - 1), skip_group_check=True)
                mm.then_inc(key_done, 1)

            def grouped(ps, diag, rows3, at, g, col_step, first, last, g_step):
                for n, (w, m) in enumerate(PAIRS):
                    lo = 2 * (w * G * W + at) + 1
                    mo = 2 * (m * W + g_step[0]) + 1
                    mm = pe.matmul(ps[:, g * H:(g + 1) * H],
                                   halves(diag)[:, lo:lo + 2 * col_step * (P - 1) + 1:2 * col_step],
                                   halves(rows3)[:, mo:mo + 2 * g_step[1] * (H - 1) + 1:2 * g_step[1]],
                                   start=first and n == 0, stop=last and n == len(PAIRS) - 1,
                                   skip_group_check=True)
                return mm

            def scores(b, part, of):
                if part == 0:
                    after(pe, bk_in, b, 16 * G)
                    after(pe, k3_ready, b)
                    after(pe, sd_ready, b - 1)
                for u in range(NU * part // of, NU * (part + 1) // of):
                    mm = grouped(ps_s, bk[:, :], k3[:, :, :].rearrange("p w n -> p (w n)"), u, u, NU,
                                 u == 0, u == NU - 1, (u, NU))
                if part == of - 1:
                    mm.then_inc(s_done, 1)

            def attend(b):
                after(pe, bv_in, b, 16 * 16)
                after(pe, a3_ready, b)
                after(pe, on_ready, b - 1)
                for g in range(NU):
                    mm = grouped(ps_a, bv[:, :], a3[:, :, :].rearrange("p w n -> p (w n)"),
                                 (g % 2) * G * W // 2 + g // 2, g, H, g == 0, g == NU - 1, (g * H, 1))
                mm.then_inc(av_done, 1)

            def turn(b):
                after(pe, on_ready, b)
                after(pe, ot_ready, b - 1)
                for c in range(C):
                    dst = ps_t[:, c * S:(c + 1) * S].rearrange("p (a q v g) -> p v q a g", a=2, q=4, v=2)
                    for v in range(2):
                        mm = pe.transpose(dst[:, v], on[:, v * D + c * P:v * D + (c + 1) * P], idn[:, :])
                mm.then_inc(t_done, 1)

            def out_proj(b):
                after(pe, wo_ready, b)
                after(pe, ot_ready, b)
                after(pe, z_ready, b - 1)
                for o in range(C):
                    for c in range(C):
                        mm = pe.matmul(ps_o[:, o * S:(o + 1) * S], wo[:, c, o * P:(o + 1) * P],
                                       ot[:, c * S:(c + 1) * S], start=(c == 0), stop=(c == C - 1),
                                       skip_group_check=True)
                mm.then_inc(o_done, 1)

            def l3_in(b, p_rows):
                after(pe, pb_ready, b)
                after(pe, x3_ready, b)
                after(pe, hid_ready, p_rows)
                after(pe, rr_ready, b - 1)
                for c in range(C):
                    mm = pe.matmul(ps_h[0:K, 0:S], pb[:, PB_U + c * K:PB_U + (c + 1) * K],
                                   x3[:, c * S:(c + 1) * S], start=(c == 0), stop=(c == C - 1))
                mm.then_inc(r_done, 1)

            def l3_out(b, p_rows):
                after(pe, rr_ready, b)
                after(pe, x1_ready, p_rows)
                after(pe, xo_ready, b - 1)
                for c in range(C):
                    mm = pe.matmul(ps_f[:, c * S:(c + 1) * S], vms[:, c * P:(c + 1) * P], rr[:, :],
                                   start=True, stop=True, skip_group_check=True)
                mm.then_inc(l3_done, 1)

            def step(i, par, do_p=False, do_s=False, do_q=False):
                p_rows = i + 2 if do_p else B - 1
                if do_q:
                    attend(i)
                if do_p:
                    down(i + 2, par)
                if do_s:
                    scores(i + 1, 0, 2)
                if do_q:
                    turn(i)
                if do_p:
                    up(i + 2)
                if do_s:
                    scores(i + 1, 1, 2)
                if do_q:
                    out_proj(i)
                if do_p:
                    l1(i + 2)
                if do_q:
                    l3_in(i, p_rows)
                    l3_out(i, p_rows)
                if do_p:
                    key(i + 2, par)

            steps(pe, step)

        @block.scalar
        def _(act):
            act.wait_ge(ld_small, 16 * N_SMALL)
            act.activation(x2[:, 0, :], w1s[:, :, :].rearrange("p c d -> p (c d)"), ACT.Square)
            act.activation(x2[:, 1, :], wos[:, :, :].rearrange("p c d -> p (c d)"), ACT.Square)
            act.activation(x3[:, :], wks[:, :, :].rearrange("p c d -> p (c d)"), ACT.Square).then_inc(su_act, 1)
            act.wait_ge(su_dve, SU_VAR)
            act.activation(dt1[:, :, :, :], dem[:, :, :, :], ACT.Sqrt)
            act.activation(rk1[:, :], rk0[:, :], ACT.Sqrt).then_inc(su_act, 1)
            act.wait_ge(su_dve, SU_U)

            def load_x(b, par):
                after(act, x1_ready, b - 2)
                act.dma_start(xin[:, par, :], xT[bass.ds(b, 1), :, :, :].rearrange("o p c s -> p (o c s)")).then_inc(x_in[par], 16)

            def load_bc(b, par):
                after(act, wk_ready, b - 2)
                after(act, wd_ready, b - 2)
                after(act, wu_ready, b - 2)
                act.dma_start(bc[:, par, :], rows_dram[bass.ds(b, 1), :].to_broadcast([P, NROW])).then_inc(bc_in[par], 16)

            def store(b, par):
                after(act, xo_ready, b)
                act.dma_start(outT[bass.ds(b, 1), :, :, :].rearrange("o p c s -> p (o c s)"), xo[:, par, :]).then_inc(out_st[par], 16)

            def make_w1(b):
                after(act, wk_ready, b - 1)
                after(act, y1_ready, b - 1)
                act.copy(pa[:, :], pa_all[:, bass.ds(b, 1), :].rearrange("p o n -> p (o n)")).then_inc(pa_ready, 1)
                after(act, pa_ready, b)
                after(act, l1_done, b - 1)
                for c in range(C):
                    ins = act.activation(w1[:, c, :], w1s[:, c, :], ACT.Copy, scale=pa[:, PA_STYLE1 + c:PA_STYLE1 + c + 1])
                ins.then_inc(w1_ready, 1)

            def make_wo(b):
                after(act, r_done, b - 1)
                after(act, rr_ready, b - 1)
                act.copy(pb[:, :], pb_all[:, bass.ds(b, 1), :].rearrange("p o n -> p (o n)")).then_inc(pb_ready, 1)
                after(act, pb_ready, b)
                after(act, o_done, b - 1)
                for c in range(C):
                    ins = act.activation(wo[:, c, :], wos[:, c, :], ACT.Copy, scale=pb[:, PB_STYLEO + c:PB_STYLEO + c + 1])
                ins.then_inc(wo_ready, 1)

            def relu(b):
                after(act, down_done, b)
                after(act, up_done, b - 1)
                act.activation(hid[:, :], ps_h[0:HID, 0:S], ACT.Relu).then_inc(hid_ready, 1)

            def y(b):
                after(act, l1_done, b)
                after(act, pa_ready, b)
                after(act, yc_ready, b - 1)
                for c in range(C):
                    ins = act.activation(y1[:, c * S:(c + 1) * S], ps_1[:, c * S:(c + 1) * S], ACT.Identity,
                                         scale=pa[:, PA_DEMOD1 + c:PA_DEMOD1 + c + 1], bias=b1s[:, c:c + 1])
                ins.then_inc(y1_ready, 1)

            def exp(b):
                after(act, sd_ready, b)
                after(act, pr_ready, b - 1)
                after(act, sum_ready, b - 1)
                act.activation(ex[:, :], sd[:, :], ACT.Exp, scale=SCALE).then_inc(ex_ready, 1)

            def take_turned(b):
                after(act, t_done, b)
                after(act, o_done, b - 1)
                act.copy(ot[:, :], ps_t[:, :]).then_inc(ot_ready, 1)

            def z(b):
                after(act, o_done, b)
                after(act, x3_ready, b - 1)
                for c in range(C):
                    ins = act.activation(zz[:, c * S:(c + 1) * S], ps_o[:, c * S:(c + 1) * S], ACT.Identity,
                                         scale=pb[:, PB_DEMODO + c:PB_DEMODO + c + 1], bias=obs[:, c:c + 1])
                ins.then_inc(z_ready, 1)

            def r(b):
                after(act, r_done, b)
                after(act, l3_done, b - 1)
                act.activation(rr[:, :], ps_h[0:K, 0:S], ACT.Identity, bias=pb[0:K, PB_ULAST:PB_ULAST + 1]).then_inc(rr_ready, 1)

            def step(i, par, do_p=False, do_s=False, do_q=False, do_load=False, do_store=True):
                if do_load:
                    load_x(i + 3, 1 - par)
                    load_bc(i + 3, 1 - par)
                if do_p:
                    make_w1(i + 2)
                if do_q:
                    make_wo(i)
                    if do_store:
                        store(i - 1, 1 - par)
                if do_p:
                    relu(i + 2)
                if do_q:
                    take_turned(i)
                if do_s:
                    exp(i + 1)
                if do_q:
                    z(i)
                if do_p:
                    y(i + 2)
                if do_q:
                    r(i)

            step(-2, 0, do_p=True)
            step(-1, 1, do_p=True, do_s=True, do_load=True)
            step(0, 0, do_p=True, do_s=True, do_q=True, do_load=True, do_store=False)
            with act.Fori(1, B - 4, 2) as i:
                step(i, 1, do_p=True, do_s=True, do_q=True, do_load=True)
                step(i + 1, 0, do_p=True, do_s=True, do_q=True, do_load=True)
            step(B - 3, 1, do_p=True, do_s=True, do_q=True)
            step(B - 2, 0, do_s=True, do_q=True)
            step(B - 1, 1, do_q=True)
            store(B - 1, 1)
            for par in range(2):
                act.wait_ge(out_st[par], 16 * B // 2)

        @block.gpsimd
        def _(pool):
            pool.memset(bk[:, :], 0.0).then_inc(zero_k, 1)
            pool.wait_ge(su_pe, 5)
            pool.memset(bv[:, :], 0.0).then_inc(zero_v, 1)

            def v_parts(b):
                after(pool, v0_ready, b)
                pool.tensor_tensor(v3[:, 1, :], v3[:, 0, :], halves(v3[:, 0, :])[:, 1::2], ALU.subtract).then_inc(v1_ready, 1)
                after(pool, v1_ready, b)
                pool.tensor_tensor(v3[:, 2, :], v3[:, 1, :], halves(v3[:, 1, :])[:, 1::2], ALU.subtract).then_inc(v3_ready, 1)

            def make_x2(b, par):
                after(pool, yc_ready, b)
                after(pool, x1_ready, b)
                after(pool, x3_ready, b - 2)
                pool.tensor_tensor(x2[:, par, :], x1[:, :], yc[:, :], ALU.add).then_inc(x2_ready, 1)

            def probs(b):
                after(pool, inv_ready, b)
                after(pool, ex_ready, b)
                after(pool, a0_ready, b - 1)
                pool.tensor_tensor(pr[:, :].rearrange("p (u j) -> p u j", j=H), ex[:, :].rearrange("p (u j) -> p u j", j=H),
                                   sinv[:, :].unsqueeze(2).to_broadcast([P, NU, H]), ALU.mult).then_inc(pr_ready, 1)

            def make_x3(b, par):
                after(pool, z_ready, b)
                after(pool, x2_ready, b)
                after(pool, r_done, b - 1)
                after(pool, xo_ready, b - 1)
                pool.tensor_tensor(x3[:, :], x2[:, par, :], zz[:, :], ALU.add).then_inc(x3_ready, 1)

            def step(i, par, do_p=False, do_s=False, do_q=False):
                if do_s:
                    v_parts(i + 1)
                if do_q:
                    make_x3(i, par)
                if do_s:
                    probs(i + 1)
                if do_p:
                    make_x2(i + 2, par)

            steps(pool, step)

        @block.vector
        def _(dve):
            count = [0]

            def setup(ins):
                count[0] += 1
                ins.then_inc(su_dve, 1)
                dve.wait_ge(su_dve, count[0])

            dve.wait_ge(su_pe, 1)
            styles = ps_h[:, 0:3 * C * B].rearrange("p (n c b) -> p n c b", n=3, c=C)
            for n in range(3):
                for c in range(C):
                    ins = dve.tensor_scalar(sty[:, n, c, :], styles[:, n, c, :], GAIN if n == 0 else 1.0,
                                            afb[:, n, c:c + 1], ALU.mult, ALU.add)
                setup(ins)
            assert count[0] == SU_STY
            setup(dve.tensor_copy(pa_all[:, :, PA_STYLE1:PA_STYLE1 + 2].rearrange("p b c -> p c b"), sty[:, 0, :, :]))
            setup(dve.tensor_tensor(sty2[:, :, :, :].rearrange("p n c b -> p (n c b)"), sty[:, :, :, :].rearrange("p n c b -> p (n c b)"),
                                    sty[:, :, :, :].rearrange("p n c b -> p (n c b)"), ALU.mult))
            assert count[0] == SU_STY2
            dve.tensor_copy(pa_all[:, :, PA_STYLEK:PA_STYLEK + 2].rearrange("p b c -> p c b"), sty[:, 1, :, :])
            dve.tensor_copy(pb_all[:, :, PB_STYLEO:PB_STYLEO + 2].rearrange("p b c -> p c b"), sty[:, 2, :, :])
            dve.wait_ge(su_pe, 3)
            dve.tensor_scalar(rk0[:, :], ps_s[0:B, 0:D], EPS, None, ALU.add)
            setup(dve.tensor_scalar(dem[:, :, :, :].rearrange("p n c b -> p (n c b)"), ps_k[:, 0:2 * C * B], EPS, None, ALU.add))
            assert count[0] == SU_VAR
            dve.wait_ge(su_act, 2)
            flat = [t[:, :, :, :].rearrange("p n c b -> p (n c b)") for t in (dem, dt1, dt2)]

            def newton(var, root, tmp, out):
                yield dve.reciprocal(tmp, root)
                yield dve.tensor_tensor(root, tmp, tmp, ALU.mult)
                yield dve.tensor_tensor(root, root, var, ALU.mult)
                yield dve.tensor_scalar(root, root, -0.5, 1.5, ALU.mult, ALU.add)
                yield dve.tensor_tensor(out, root, tmp, ALU.mult)

            rkd = rows[:, R_DK:R_DK + D]
            dve.tensor_copy(rows[:, 0:2 * HID], ps_f[0:B, 0:2 * HID])
            dve.tensor_copy(rows[:, R_UG:R_UG + 2 * D], ps_1[0:B, :])
            for ins in newton(rk0[:, :], rk1[:, :], kx[0:B, 0:D], rkd):
                setup(ins)
            assert count[0] == SU_ROWS
            for ins in newton(flat[0], flat[1], flat[2], flat[0]):
                setup(ins)
            dve.tensor_copy(pa_all[:, :, PA_DEMOD1:PA_DEMOD1 + 2].rearrange("p b c -> p c b"), dem[:, 0, :, :])
            dve.tensor_copy(pb_all[:, :, PB_DEMODO:PB_DEMODO + 2].rearrange("p b c -> p c b"), dem[:, 1, :, :])
            dve.wait_ge(su_pe, 4)
            banks = (ps_a, ps_t, ps_o, ps_h)
            for c in range(C):
                for half in range(2):
                    k0, k1 = 16 * half, min(K, 16 * half + 16)
                    src = banks[2 * c + half][:, 0:(k1 - k0) * B].rearrange("p (k b) -> p k b", b=B)
                    dst = pb_all[:, :, PB_U + c * K + k0:PB_U + c * K + k1].rearrange("p b k -> p k b")
                    dve.tensor_tensor(dst, src, bds[:, c, k0:k1].unsqueeze(2).to_broadcast([P, k1 - k0, B]), ALU.add)
            setup(dve.memset(pb_all[:, :, PB_ULAST:PB_ULAST + 1], 0.0))
            dve.wait_ge(su_pe, 5)
            setup(dve.tensor_scalar(pb_all[0:K, :, PB_ULAST], ps_k[0:K, 0:B], bdl[:, 0:1], None, ALU.add))
            assert count[0] == SU_U

            def make_weights(b, par):
                dve.wait_ge(bc_in[par], pair_count(b, par))
                row = bc[:, par, :]
                after(dve, down_done, b - 1)
                both = [P, C, HID]
                dve.tensor_tensor(wd[:, :, :], dpj[:, :, :], row[:, R_DG:R_DG + HID].unsqueeze(1).to_broadcast(both),
                                  ALU.mult).then_inc(wd_half, 1)
                after(dve, up_done, b - 1)
                dve.tensor_tensor(wu[:, :], upj[:, :], row[0:HID, R_UG:R_UG + D], ALU.mult).then_inc(wu_half, 1)
                after(dve, wd_half, b)
                dve.tensor_tensor(wd[:, :, :], wd[:, :, :], row[:, R_DB:R_DB + HID].unsqueeze(1).to_broadcast(both),
                                  ALU.add).then_inc(wd_ready, 1)
                after(dve, wu_half, b)
                dve.tensor_tensor(wu[:, :], wu[:, :], row[0:HID, R_UB:R_UB + D], ALU.add).then_inc(wu_ready, 1)

            def make_wk(b, par):
                after(dve, pa_ready, b)
                after(dve, key_done, b - 1)
                for c in range(C):
                    ins = dve.scalar_tensor_tensor(out=wk[:, c, :], in0=wks[:, c, :], scalar=pa[:, PA_STYLEK + c:PA_STYLEK + c + 1],
                                                   in1=bc[:, par, R_DK:R_DK + D], op0=ALU.mult, op1=ALU.mult)
                ins.then_inc(wk_ready, 1)

            def make_x1(b, par):
                after(dve, up_done, b)
                after(dve, l1_done, b - 1)
                after(dve, x2_ready, b - 1)
                dve.scalar_tensor_tensor(out=x1[:, :], in0=xin[:, par, :], scalar=2.0, in1=ps_f[:, :],
                                         op0=ALU.mult, op1=ALU.add).then_inc(x1_ready, 1)

            def clip(b):
                after(dve, y1_ready, b)
                after(dve, x2_ready, b - 1)
                dve.tensor_scalar(yc[:, :], y1[:, :], -CLAMP, CLAMP, ALU.max, ALU.min).then_inc(yc_ready, 1)

            def keys(b):
                after(dve, key_done, b)
                kxa = kx[:, :].rearrange("p (a n) -> p a n", a=2)
                dve.tensor_tensor(kxa, ps_k[:, :].rearrange("p (a n) -> p a n", a=2),
                                  kbs[:, :].unsqueeze(1).to_broadcast([P, 2, D]), ALU.add).then_inc(kx_ready, 1)
                after(dve, kx_ready, b)
                after(dve, s_done, b - 1)
                dve.transpose(k3[:, 0, :], kx[:, :].rearrange("p (a h d) -> p h a d", a=2, h=H)).then_inc(k0_ready, 1)
                after(dve, bv_in, b - 1, 16 * 16)
                dve.transpose(v3[:, 0, :].rearrange("p (v d g) -> p d v g", v=2, d=DH),
                              kx[:, :].rearrange("p (a j d) -> p d a j", a=2, j=H)).then_inc(v0_ready, 1)
                after(dve, k0_ready, b)
                dve.tensor_tensor(k3[:, 1, :], k3[:, 0, :], halves(k3[:, 0, :])[:, 1::2], ALU.subtract).then_inc(k1_ready, 1)
                after(dve, k1_ready, b)
                dve.tensor_tensor(k3[:, 2, :], k3[:, 1, :], halves(k3[:, 1, :])[:, 1::2], ALU.subtract).then_inc(k3_ready, 1)

            def softmax_shift(b):
                after(dve, s_done, b)
                scores = ps_s[:, :].rearrange("p (u j) -> p u j", j=H)
                dve.tensor_reduce(smax[:, :], scores, AX.X, ALU.max).then_inc(max_ready, 1)
                after(dve, max_ready, b)
                after(dve, ex_ready, b - 1)
                dve.tensor_tensor(sd[:, :].rearrange("p (u j) -> p u j", j=H), scores,
                                  smax[:, :].unsqueeze(2).to_broadcast([P, NU, H]), ALU.subtract).then_inc(sd_ready, 1)

            def softmax_sum(b):
                after(dve, ex_ready, b)
                dve.tensor_reduce(ssum[:, :], ex[:, :].rearrange("p (u j) -> p u j", j=H), AX.X, ALU.add).then_inc(sum_ready, 1)
                after(dve, sum_ready, b)
                after(dve, pr_ready, b - 1)
                dve.reciprocal(sinv[:, :], ssum[:, :]).then_inc(inv_ready, 1)

            def prob_parts(b):
                after(dve, pr_ready, b)
                after(dve, av_done, b - 1)
                dve.transpose(a3[:, 0, :], pr[:, :].rearrange("p (v g j) -> p g v j", v=2, j=H)).then_inc(a0_ready, 1)
                after(dve, a0_ready, b)
                dve.tensor_tensor(a3[:, 1, :], a3[:, 0, :], halves(a3[:, 0, :])[:, 1::2], ALU.subtract).then_inc(a1_ready, 1)
                after(dve, a1_ready, b)
                dve.tensor_tensor(a3[:, 2, :], a3[:, 1, :], halves(a3[:, 1, :])[:, 1::2], ALU.subtract).then_inc(a3_ready, 1)

            def turn_attended(b):
                after(dve, av_done, b)
                after(dve, t_done, b - 1)
                dve.transpose(on[:, :].rearrange("p (v h d) -> p h v d", v=2, h=H),
                              ps_a[:, :].rearrange("p (g a h) -> p h a g", a=2, h=H)).then_inc(on_ready, 1)

            def make_out(b, par):
                after(dve, l3_done, b)
                after(dve, x3_ready, b)
                if not isinstance(b, int) or b >= 2:
                    dve.wait_ge(out_st[par], (b - par) * 8)
                dve.tensor_tensor(xo[:, par, :], x3[:, :], ps_f[:, :], ALU.add).then_inc(xo_ready, 1)

            def step(i, par, do_p=False, do_s=False, do_q=False):
                if do_s:
                    keys(i + 1)
                if do_p:
                    make_weights(i + 2, par)
                if do_q:
                    turn_attended(i)
                if do_p:
                    make_wk(i + 2, par)
                    make_x1(i + 2, par)
                if do_s:
                    softmax_shift(i + 1)
                if do_p:
                    clip(i + 2)
                if do_s:
                    softmax_sum(i + 1)
                if do_q:
                    make_out(i, par)
                if do_s:
                    prob_parts(i + 1)

            steps(dve, step)


def kernel(x, cond_512, L0_cond_down_project, L0_cond_down_gamma, L0_cond_down_beta, L0_cond_up_project,
           L0_cond_up_gamma, L0_cond_up_beta, L1_cond_weight, L1_cond_bias, L1_cond_affine_w, L1_cond_affine_b,
           L2_cond_k_aff_w, L2_cond_k_aff_b, L2_cond_k_w, L2_cond_k_b, L2_cond_o_aff_w, L2_cond_o_aff_b,
           L2_cond_o_w, L2_cond_o_b, L3_cond_W_dec, L3_cond_b_dec, L3_cond_V):
    import numpy as _np
    import concourse.bacc as _bacc
    from concourse import mybir as _mybir
    from concourse.bass_utils import run_bass_kernel_spmd as _run

    B, S, D = x.shape
    K = L3_cond_V.shape[0]

    def chunks(w):
        w = _np.asarray(w)
        return w.reshape(D // 128, 128, -1).transpose(1, 0, 2)

    def column(v):
        return _np.asarray(v).reshape(D // 128, 128).T

    arrays = {
        "xT": _np.asarray(x).transpose(0, 2, 1).reshape(B, D // 128, 128, S).transpose(0, 2, 1, 3),
        "condT": _np.asarray(cond_512).T,
        "gb_down": _np.concatenate([_np.asarray(L0_cond_down_gamma), _np.asarray(L0_cond_down_beta)], 1),
        "gb_up": _np.concatenate([_np.asarray(L0_cond_up_gamma), _np.asarray(L0_cond_up_beta)], 1),
        "dproj": chunks(L0_cond_down_project),
        "uproj": _np.asarray(L0_cond_up_project),
        "w1T": chunks(_np.asarray(L1_cond_weight).T),
        "bias1": column(L1_cond_bias),
        "aff1T": _np.asarray(L1_cond_affine_w).T,
        "affb1": column(L1_cond_affine_b),
        "wkT": chunks(_np.asarray(L2_cond_k_w).T),
        "affkT": _np.asarray(L2_cond_k_aff_w).T,
        "affbk": column(L2_cond_k_aff_b),
        "kb": _np.asarray(L2_cond_k_b).reshape(1, D),
        "woT": chunks(_np.asarray(L2_cond_o_w).T),
        "affoT": _np.asarray(L2_cond_o_aff_w).T,
        "affbo": column(L2_cond_o_aff_b),
        "ob": column(L2_cond_o_b),
        "wdec": _np.asarray(L3_cond_W_dec),
        "bdec": chunks(_np.asarray(L3_cond_b_dec)[:D * K].reshape(D, K)),
        "bdec_last": _np.asarray(L3_cond_b_dec)[D * K:].reshape(K, 1),
        "vmat": _np.asarray(L3_cond_V),
        "ident": _np.eye(128, dtype=_np.float32),
    }
    arrays = {n: _np.ascontiguousarray(a) for n, a in arrays.items()}
    nc = _bacc.Bacc("TRN2", target_bir_lowering=False, num_devices=1)
    args = [nc.dram_tensor(n, a.shape, _mybir.dt.from_np(a.dtype), kind="ExternalInput").ap() for n, a in arrays.items()]
    args.append(nc.dram_tensor("outT", arrays["xT"].shape, _mybir.dt.float32, kind="ExternalOutput").ap())
    build(nc, *args)
    r = _run(nc, [arrays], core_ids=[0])
    out = _np.asarray(r.results[0]["outT"])
    return out.transpose(0, 2, 1, 3).reshape(B, D, S).transpose(0, 2, 1)
```

```python
from contextlib import ExitStack

import numpy as np

import concourse.bass as bass
from concourse import mybir

F32 = mybir.dt.float32
BF16 = mybir.dt.bfloat16
ALU = mybir.AluOpType
ACT = mybir.ActivationFunctionType
AX = mybir.AxisListType

P = 128
C = 2
H, DH = 16, 16
G = 8
NU = 32
CLAMP = 256.0
EPS = 1e-8
PARTS = 3
UNROLL = 4
PER_BANK = 8

PA_STYLE1, PA_STYLEK, PA_DEMOD1, PA_N = 0, 2, 4, 6
PB_STYLEO, PB_DEMODO, PB_ULAST, PB_U = 0, 2, 4, 5


def build(nc, xT, condT, gb_down, gb_up, dproj, uproj, w1T, bias1, aff1T, affb1, wkT, affkT, affbk, kb,
          woT, affoT, affbo, ob, wdec, bdec, bdec_last, vmat, ident, outT):
    B, _, _, S = xT.shape
    D = C * P
    HID = uproj.shape[0]
    K = vmat.shape[0]
    CD = condT.shape[0]
    GAIN = float(np.float32(1.0) / np.sqrt(CD).astype(np.float32))
    SCALE = 1.0 / float(np.sqrt(DH))
    PB_N = PB_U + C * K
    NROW = 2 * HID + 2 * D + D
    R_DG, R_DB, R_UG, R_UB, R_DK = 0, HID, 2 * HID, 2 * HID + D, 2 * HID + 2 * D
    W = C * S
    assert W == 512 and S == 2 * P and D == H * DH

    with ExitStack() as ctx:
        def sb(name, shape, dt=F32):
            return ctx.enter_context(nc.sbuf_tensor(name, shape, dt))

        def psum(name):
            return ctx.enter_context(nc.psum_tensor(name, [P, W], F32))

        def sem(name):
            return ctx.enter_context(nc.semaphore(name))

        rows_dram = nc.dram_tensor("rows_dram", [B, NROW], F32).ap()

        cond = sb("cond", [CD, B])
        dpj, upj = sb("dpj", [P, C, HID]), sb("upj", [HID, D])
        w1s, wks, wos = sb("w1s", [P, C, D]), sb("wks", [P, C, D]), sb("wos", [P, C, D])
        afb = sb("afb", [P, 3, C])
        b1s, obs = sb("b1s", [P, C]), sb("obs", [P, C])
        kbs = sb("kbs", [P, D])
        bds, bdl = sb("bds", [P, C, K]), sb("bdl", [K, 1])
        vms = sb("vms", [K, D])
        idn = sb("idn", [P, P])
        rows = sb("rows", [B, NROW])
        pa_all, pb_all = sb("pa_all", [P, B, PA_N]), sb("pb_all", [P, B, PB_N])
        sty = sb("sty", [P, 3, C, B])
        sty2 = sb("sty2", [P, 3, C, B])
        dem = sb("dem", [P, 2, C, B])
        dt1, dt2 = sb("dt1", [P, 2, C, B]), sb("dt2", [P, 2, C, B])
        rk0, rk1 = sb("rk0", [B, D]), sb("rk1", [B, D])
        bc = sb("bc", [P, 2, NROW])
        pa, pb = sb("pa", [P, PA_N]), sb("pb", [P, PB_N])
        wd, wu = sb("wd", [P, C, HID]), sb("wu", [HID, D])
        w1, wk, wo = sb("w1", [P, C, D]), sb("wk", [P, C, D]), sb("wo", [P, C, D])
        xin = sb("xin", [P, 2, W])
        hid = sb("hid", [HID, S])
        x1, y1, yc = sb("x1", [P, W]), sb("y1", [P, W]), sb("yc", [P, W])
        x2 = sb("x2", [P, UNROLL, W])
        kx = sb("kx", [P, 2, W])
        k3 = sb("k3", [P, 2, PARTS, W])
        v3, a3 = sb("v3", [P, PARTS, W]), sb("a3", [P, PARTS, W])
        bk, bv = sb("bk", [P, PARTS * G * W]), sb("bv", [P, PARTS * G * W])
        smax, ssum, sinv = sb("smax", [P, NU]), sb("ssum", [P, NU]), sb("sinv", [P, NU])
        sc, ex, pr = sb("sc", [P, W]), sb("ex", [P, W]), sb("pr", [P, W])
        av, on, ot = sb("av", [P, W]), sb("on", [P, W]), sb("ot", [P, W])
        zz, x3 = sb("zz", [P, W]), sb("x3", [P, W])
        rr = sb("rr", [K, S])
        xo = sb("xo", [P, 2, W])
        at = (D + 1) * K
        wds = bv[:, 0:at]
        afs = [bv[0:CD, at + n * D:at + (n + 1) * D] for n in range(3)]
        at += 3 * D
        gbd, gbu = bv[0:CD, at:at + 2 * HID], bv[0:CD, at + 2 * HID:at + 2 * HID + 2 * D]

        ps_h, ps_f, ps_1, ps_k = (psum(n) for n in ("ps_h", "ps_f", "ps_1", "ps_k"))
        ps_t, ps_o = ps_1, ps_k
        ps_g = ctx.enter_context(nc.psum_tensor("ps_g", [P, NU // PER_BANK, W], F32))
        magnitude = ps_g[:, :, 0:PER_BANK * PARTS * H].rearrange("p b (u m h) -> p m b u h", u=PER_BANK, m=PARTS)

        ld_small = sem("ld_small")
        ld_wdec = sem("ld_wdec")
        rows_out = sem("rows_out")
        x_in = [sem("x_in0"), sem("x_in1")]
        bc_in = [sem("bc_in0"), sem("bc_in1")]
        out_st = [sem("out_st0"), sem("out_st1")]
        bk_in, bv_in = sem("bk_in"), sem("bv_in")
        bv_pool = sem("bv_pool")
        zero_k, zero_v = sem("zero_k"), sem("zero_v")
        su_pe, su_act, su_dve = sem("su_pe"), sem("su_act"), sem("su_dve")
        pa_ready, pb_ready, w1_ready, wo_ready = sem("pa_ready"), sem("pb_ready"), sem("w1_ready"), sem("wo_ready")
        wd_half, wu_half = sem("wd_half"), sem("wu_half")
        wd_ready, wu_ready, wk_ready = sem("wd_ready"), sem("wu_ready"), sem("wk_ready")
        down_done, up_done, l1_done, key_done = sem("down_done"), sem("up_done"), sem("l1_done"), sem("key_done")
        hid_ready, x1_ready, y1_ready, yc_ready, x2_ready = (
            sem("hid_ready"), sem("x1_ready"), sem("y1_ready"), sem("yc_ready"), sem("x2_ready"))
        kx_ready, k0_ready, k1_ready, k3_ready = sem("kx_ready"), sem("k0_ready"), sem("k1_ready"), sem("k3_ready")
        v0_ready, v1_ready, v3_ready = sem("v0_ready"), sem("v1_ready"), sem("v3_ready")
        s_done, max_ready, sd_ready, ex_ready = sem("s_done"), sem("max_ready"), sem("sd_ready"), sem("ex_ready")
        slo_ready, smid_ready, sc_ready = sem("slo_ready"), sem("smid_ready"), sem("sc_ready")
        alo_ready, amid_ready, av_ready = sem("alo_ready"), sem("amid_ready"), sem("av_ready")
        sum_ready, inv_ready, pr_ready = sem("sum_ready"), sem("inv_ready"), sem("pr_ready")
        a0_ready, a1_ready, a3_ready = sem("a0_ready"), sem("a1_ready"), sem("a3_ready")
        av_done, on_ready, t_done, ot_ready = sem("av_done"), sem("on_ready"), sem("t_done"), sem("ot_ready")
        o_done, z_ready, x3_ready = sem("o_done"), sem("z_ready"), sem("x3_ready")
        r_done, rr_ready, l3_done, xo_ready = sem("r_done"), sem("rr_ready"), sem("l3_done"), sem("xo_ready")

        def after(eng, s, b, per=1):
            if isinstance(b, int) and b < 0:
                return
            eng.wait_ge(s, (b + 1) * per if per > 1 else b + 1)

        def pair_count(b, par):
            return (b - par) * 8 + 16

        VALUE_BLOCKS = [(32 * q + 16 * v, 32 * q + 16 * a, a, v) for q in range(4) for v in range(2) for a in range(2)]
        ON_POOL = 5

        def halves(t):
            return t.bitcast(BF16)

        N_SMALL = 21
        SU_STY, SU_STY2, SU_VAR, SU_ROWS, SU_U = 3, 5, 6, 11, 18
        FIRST, LAST = 4, 28
        assert B % UNROLL == 0 and LAST + 3 < B

        def has(b):
            return not isinstance(b, int) or 0 <= b < B

        def steps(eng, step):
            for i in range(-4, FIRST):
                step(i, i % UNROLL)
            with eng.Fori(FIRST, LAST - UNROLL + 1, UNROLL) as i:
                for j in range(UNROLL):
                    step(i + j, j)
            for i in range(LAST, B + 1):
                step(i, i % UNROLL)

        block = ctx.enter_context(nc.Block())

        @block.sync
        def _(sp):
            small = [(cond[:, :], condT), (afs[0], aff1T), (afs[1], affkT), (afs[2], affoT),
                     (afb[:, 0, :], affb1), (afb[:, 1, :], affbk), (afb[:, 2, :], affbo),
                     (w1s[:, :, :], w1T), (wks[:, :, :], wkT), (wos[:, :, :], woT),
                     (gbd, gb_down), (gbu, gb_up),
                     (dpj[:, :, :], dproj), (upj[:, :], uproj), (b1s[:, :], bias1), (obs[:, :], ob),
                     (kbs[:, :], kb.to_broadcast([P, D])), (bds[:, :, :], bdec), (bdl[:, :], bdec_last),
                     (vms[:, :], vmat), (idn[:, :], ident)]
            assert len(small) == N_SMALL
            for dst, src in small:
                sp.dma_start(dst, src).then_inc(ld_small, 16)
            sp.dma_start(wds, wdec).then_inc(ld_wdec, 16)
            sp.dma_start(xin[:, 0, :], xT[0].rearrange("p c s -> p (c s)")).then_inc(x_in[0], 16)
            sp.dma_start(xin[:, 1, :], xT[1].rearrange("p c s -> p (c s)")).then_inc(x_in[1], 16)
            sp.wait_ge(su_dve, SU_ROWS)
            sp.dma_start(rows_dram, rows[:, :]).then_inc(rows_out, 16)
            sp.wait_ge(rows_out, 16)
            for b in range(2):
                sp.dma_start(bc[:, b, :], rows_dram[b:b + 1, :].to_broadcast([P, NROW])).then_inc(bc_in[b], 16)

            def keys_to_diagonal(b, slot):
                after(sp, k3_ready, b)
                after(sp, s_done, b - 1)
                dst = bk[:, :].rearrange("p (w t n) -> p w t n", w=PARTS, t=G)
                for t in range(G):
                    sp.dma_start(dst[16 * t:16 * t + 16, :, t, :], k3[16 * t:16 * t + 16, slot, :, :]).then_inc(bk_in, 16)

            def values_to_diagonal(b):
                after(sp, av_done, b - 1)
                after(sp, v3_ready, b)
                dst = bv[:, :].rearrange("p (w a t n) -> p w a t n", w=PARTS, a=2, t=G)
                src = v3[:, :, :].rearrange("p w (v n) -> p w v n", v=2)
                for to, at, a, v in VALUE_BLOCKS[ON_POOL:]:
                    sp.dma_start(dst[to:to + 16, :, a, to // 16, :], src[at:at + 16, :, v, :]).then_inc(bv_in, 16)

            sp.wait_ge(zero_k, 1)
            keys_to_diagonal(0, 0)
            sp.wait_ge(zero_v, 1)
            values_to_diagonal(0)
            keys_to_diagonal(1, 1)
            with sp.Fori(2, B - 1, 2) as b:
                keys_to_diagonal(b, 0)
                values_to_diagonal(b - 1)
                keys_to_diagonal(b + 1, 1)
                values_to_diagonal(b)
            values_to_diagonal(B - 1)

        @block.tensor
        def _(pe):
            pe.wait_ge(ld_small, 16 * N_SMALL)
            for n in range(3):
                for c in range(C):
                    mm = pe.matmul(ps_h[:, (n * C + c) * B:(n * C + c + 1) * B], afs[n][:, c * P:(c + 1) * P],
                                   cond[:, :], start=True, stop=True, skip_group_check=True)
            mm.then_inc(su_pe, 1)
            pe.matmul(ps_f[0:B, 0:2 * HID], cond[:, :], gbd, start=True, stop=True)
            pe.matmul(ps_1[0:B, :], cond[:, :], gbu, start=True, stop=True).then_inc(su_pe, 1)
            pe.wait_ge(su_act, 1)
            pe.wait_ge(su_dve, SU_STY2)
            for n, sq in ((0, x2[:, 0, :]), (1, x2[:, 1, :])):
                for o in range(C):
                    for c in range(C):
                        mm = pe.matmul(ps_k[:, (n * C + o) * B:(n * C + o + 1) * B],
                                       sq[:, c * D + o * P:c * D + (o + 1) * P], sty2[:, 2 * n, c, :],
                                       start=(c == 0), stop=(c == C - 1), skip_group_check=True)
            for c in range(C):
                mm = pe.matmul(ps_g[0:B, 0, 0:D], sty2[:, 1, c, :], x3[:, c * D:(c + 1) * D],
                               start=(c == 0), stop=(c == C - 1))
            mm.then_inc(su_pe, 1)
            pe.wait_ge(ld_wdec, 16)
            banks = (ps_g[:, 1, :], ps_g[:, 2, :], ps_g[:, 3, :], ps_h[:, :])
            for c in range(C):
                for k in range(K):
                    bank, at = banks[2 * c + k // 16], (k % 16) * B
                    mm = pe.matmul(bank[:, at:at + B], wds[:, c * P * K + k:c * P * K + k + (P - 1) * K + 1:K],
                                   cond[:, :], start=True, stop=True, skip_group_check=True)
            mm.then_inc(su_pe, 1)
            pe.wait_ge(su_dve, SU_VAR)
            pe.matmul(ps_k[0:K, 0:B], wds[:, D * K:(D + 1) * K], cond[:, :], start=True, stop=True).then_inc(su_pe, 1)
            pe.wait_ge(su_dve, SU_U)

            def last_row(b):
                return min(b, B - 1) if isinstance(b, int) else b

            def down(b, par):
                after(pe, wd_ready, b)
                pe.wait_ge(x_in[par], pair_count(b, par))
                after(pe, hid_ready, b - 1)
                after(pe, rr_ready, b - 5)
                for c in range(C):
                    mm = pe.matmul(ps_h[0:HID, 0:S], wd[:, c, :], xin[:, par, c * S:(c + 1) * S],
                                   start=(c == 0), stop=(c == C - 1))
                mm.then_inc(down_done, 1)

            def up(b):
                after(pe, wu_ready, b)
                after(pe, hid_ready, b)
                after(pe, x1_ready, b - 1)
                after(pe, xo_ready, b - 5)
                for c in range(C):
                    mm = pe.matmul(ps_f[:, c * S:(c + 1) * S], wu[:, c * P:(c + 1) * P], hid[:, :],
                                   start=True, stop=True, skip_group_check=True)
                mm.then_inc(up_done, 1)

            def l1(b):
                after(pe, w1_ready, b)
                after(pe, x1_ready, b)
                after(pe, y1_ready, b - 1)
                after(pe, ot_ready, b - 4)
                for o in range(C):
                    for c in range(C):
                        mm = pe.matmul(ps_1[:, o * S:(o + 1) * S], w1[:, c, o * P:(o + 1) * P],
                                       x1[:, c * S:(c + 1) * S], start=(c == 0), stop=(c == C - 1),
                                       skip_group_check=True)
                mm.then_inc(l1_done, 1)

            def key(b, slot):
                after(pe, wk_ready, b)
                after(pe, x2_ready, b)
                after(pe, kx_ready, b - 1)
                after(pe, z_ready, b - 4)
                for a in range(2):
                    for c in range(C):
                        mm = pe.matmul(ps_k[:, a * D:(a + 1) * D], x2[:, slot, c * S + a * P:c * S + (a + 1) * P],
                                       wk[:, c, :], start=(c == 0), stop=(c == C - 1), skip_group_check=True)
                mm.then_inc(key_done, 1)

            def grouped(g, diag, at, col_step, rows3, row_at, row_step):
                diag, rows3 = halves(diag), halves(rows3)
                for w in range(PARTS):
                    lo = 2 * (w * G * W + at) + 1
                    moving = rows3[:, 0:PARTS - w, 2 * row_at + 1:2 * (row_at + row_step * (H - 1)) + 2:2 * row_step]
                    out = ps_g[:, g // PER_BANK, (g % PER_BANK) * PARTS * H + w * H:(g % PER_BANK + 1) * PARTS * H]
                    mm = pe.matmul(out, diag[:, lo:lo + 2 * col_step * (P - 1) + 1:2 * col_step], moving,
                                   start=(g % PER_BANK == 0 and w == 0), stop=(g % PER_BANK == PER_BANK - 1 and w == PARTS - 1),
                                   skip_group_check=True)
                return mm

            def scores(b, slot):
                after(pe, bk_in, b, 16 * G)
                after(pe, k3_ready, b)
                after(pe, av_ready, b - 2)
                for u in range(NU):
                    mm = grouped(u, bk[:, :], u, NU, k3[:, slot, :, :], u, NU)
                mm.then_inc(s_done, 1)

            def attend(b):
                after(pe, bv_in, b, 16 * (16 - ON_POOL))
                after(pe, bv_pool, b, 16 * ON_POOL)
                after(pe, a3_ready, b)
                after(pe, sc_ready, last_row(b + 1))
                for g in range(NU):
                    mm = grouped(g, bv[:, :], (g % 2) * G * W // 2 + g // 2, H, a3[:, :, :], g * H, 1)
                mm.then_inc(av_done, 1)

            def turn(b):
                after(pe, on_ready, b)
                after(pe, ot_ready, b - 1)
                after(pe, y1_ready, last_row(b + 3))
                for c in range(C):
                    dst = ps_t[:, c * S:(c + 1) * S].rearrange("p (a q v g) -> p v q a g", a=2, q=4, v=2)
                    for v in range(2):
                        mm = pe.transpose(dst[:, v], on[:, v * D + c * P:v * D + (c + 1) * P], idn[:, :])
                mm.then_inc(t_done, 1)

            def out_proj(b):
                after(pe, wo_ready, b)
                after(pe, ot_ready, b)
                after(pe, z_ready, b - 1)
                after(pe, kx_ready, last_row(b + 3))
                for o in range(C):
                    for c in range(C):
                        mm = pe.matmul(ps_o[:, o * S:(o + 1) * S], wo[:, c, o * P:(o + 1) * P],
                                       ot[:, c * S:(c + 1) * S], start=(c == 0), stop=(c == C - 1),
                                       skip_group_check=True)
                mm.then_inc(o_done, 1)

            def l3_in(b):
                after(pe, pb_ready, b)
                after(pe, x3_ready, b)
                after(pe, hid_ready, last_row(b + 4))
                after(pe, rr_ready, b - 1)
                for c in range(C):
                    mm = pe.matmul(ps_h[0:K, 0:S], pb[:, PB_U + c * K:PB_U + (c + 1) * K],
                                   x3[:, c * S:(c + 1) * S], start=(c == 0), stop=(c == C - 1))
                mm.then_inc(r_done, 1)

            def l3_out(b):
                after(pe, rr_ready, b)
                after(pe, x1_ready, last_row(b + 4))
                after(pe, xo_ready, b - 1)
                for c in range(C):
                    mm = pe.matmul(ps_f[:, c * S:(c + 1) * S], vms[:, c * P:(c + 1) * P], rr[:, :],
                                   start=True, stop=True, skip_group_check=True)
                mm.then_inc(l3_done, 1)

            def step(i, j):
                if has(i + 1):
                    scores(i + 1, (j + 1) % 2)
                if has(i + 3):
                    l1(i + 3)
                if has(i - 1):
                    l3_in(i - 1)
                if has(i):
                    attend(i)
                if has(i + 3):
                    key(i + 3, (j + 3) % UNROLL)
                if has(i - 1):
                    l3_out(i - 1)
                if has(i + 4):
                    down(i + 4, j % 2)
                if has(i):
                    turn(i)
                if has(i + 4):
                    up(i + 4)
                if has(i):
                    out_proj(i)

            steps(pe, step)

        @block.scalar
        def _(act):
            act.wait_ge(ld_small, 16 * N_SMALL)
            act.activation(x2[:, 0, :], w1s[:, :, :].rearrange("p c d -> p (c d)"), ACT.Square)
            act.activation(x2[:, 1, :], wos[:, :, :].rearrange("p c d -> p (c d)"), ACT.Square)
            act.activation(x3[:, :], wks[:, :, :].rearrange("p c d -> p (c d)"), ACT.Square).then_inc(su_act, 1)
            act.wait_ge(su_dve, SU_VAR)
            act.activation(dt1[:, :, :, :], dem[:, :, :, :], ACT.Sqrt)
            act.activation(rk1[:, :], rk0[:, :], ACT.Sqrt).then_inc(su_act, 1)
            act.wait_ge(su_dve, SU_U)

            def load_x(b, par):
                after(act, x1_ready, b - 2)
                act.dma_start(xin[:, par, :], xT[bass.ds(b, 1), :, :, :].rearrange("o p c s -> p (o c s)")).then_inc(x_in[par], 16)

            def load_bc(b, par):
                after(act, wk_ready, b - 2)
                after(act, wd_ready, b - 2)
                after(act, wu_ready, b - 2)
                act.dma_start(bc[:, par, :], rows_dram[bass.ds(b, 1), :].to_broadcast([P, NROW])).then_inc(bc_in[par], 16)

            def store(b, par):
                after(act, xo_ready, b)
                act.dma_start(outT[bass.ds(b, 1), :, :, :].rearrange("o p c s -> p (o c s)"), xo[:, par, :]).then_inc(out_st[par], 16)

            def make_w1(b):
                after(act, wk_ready, b - 1)
                after(act, y1_ready, b - 1)
                act.copy(pa[:, :], pa_all[:, bass.ds(b, 1), :].rearrange("p o n -> p (o n)")).then_inc(pa_ready, 1)
                after(act, pa_ready, b)
                after(act, l1_done, b - 1)
                for c in range(C):
                    ins = act.activation(w1[:, c, :], w1s[:, c, :], ACT.Copy, scale=pa[:, PA_STYLE1 + c:PA_STYLE1 + c + 1])
                ins.then_inc(w1_ready, 1)

            def make_wo(b):
                after(act, r_done, b - 1)
                after(act, rr_ready, b - 1)
                act.copy(pb[:, :], pb_all[:, bass.ds(b, 1), :].rearrange("p o n -> p (o n)")).then_inc(pb_ready, 1)
                after(act, pb_ready, b)
                after(act, o_done, b - 1)
                for c in range(C):
                    ins = act.activation(wo[:, c, :], wos[:, c, :], ACT.Copy, scale=pb[:, PB_STYLEO + c:PB_STYLEO + c + 1])
                ins.then_inc(wo_ready, 1)

            def relu(b):
                after(act, down_done, b)
                after(act, up_done, b - 1)
                act.activation(hid[:, :], ps_h[0:HID, 0:S], ACT.Relu).then_inc(hid_ready, 1)

            def y(b):
                after(act, l1_done, b)
                after(act, pa_ready, b)
                after(act, yc_ready, b - 1)
                for c in range(C):
                    ins = act.activation(y1[:, c * S:(c + 1) * S], ps_1[:, c * S:(c + 1) * S], ACT.Identity,
                                         scale=pa[:, PA_DEMOD1 + c:PA_DEMOD1 + c + 1], bias=b1s[:, c:c + 1])
                ins.then_inc(y1_ready, 1)

            def least(out, done, ready, b):
                after(act, done, b)
                act.copy(out[:, :].rearrange("p (b u h) -> p b u h", b=NU // PER_BANK, u=PER_BANK),
                         magnitude[:, PARTS - 1]).then_inc(ready, 1)

            def least_scores(b):
                after(act, ex_ready, b - 1)
                least(sc, s_done, slo_ready, b)

            def least_attended(b):
                after(act, on_ready, b - 1)
                least(av, av_done, alo_ready, b)

            def exp(b):
                after(act, sd_ready, b)
                after(act, pr_ready, b - 1)
                after(act, sum_ready, b - 1)
                act.activation(ex[:, :], sc[:, :], ACT.Exp, scale=SCALE).then_inc(ex_ready, 1)

            def take_turned(b):
                after(act, t_done, b)
                after(act, o_done, b - 1)
                act.copy(ot[:, :], ps_t[:, :]).then_inc(ot_ready, 1)

            def z(b):
                after(act, o_done, b)
                after(act, x3_ready, b - 1)
                for c in range(C):
                    ins = act.activation(zz[:, c * S:(c + 1) * S], ps_o[:, c * S:(c + 1) * S], ACT.Identity,
                                         scale=pb[:, PB_DEMODO + c:PB_DEMODO + c + 1], bias=obs[:, c:c + 1])
                ins.then_inc(z_ready, 1)

            def r(b):
                after(act, r_done, b)
                after(act, l3_done, b - 1)
                act.activation(rr[:, :], ps_h[0:K, 0:S], ACT.Identity, bias=pb[0:K, PB_ULAST:PB_ULAST + 1]).then_inc(rr_ready, 1)

            def step(i, j):
                if has(i + 4) and (not isinstance(i, int) or i + 4 >= 2):
                    load_x(i + 4, j % 2)
                    load_bc(i + 4, j % 2)
                if has(i - 1):
                    z(i - 1)
                if has(i + 1):
                    least_scores(i + 1)
                if has(i + 3):
                    y(i + 3)
                if has(i - 1):
                    r(i - 1)
                if has(i + 1):
                    exp(i + 1)
                if has(i):
                    make_wo(i)
                if has(i + 4):
                    make_w1(i + 4)
                if has(i):
                    least_attended(i)
                if has(i + 4):
                    relu(i + 4)
                if has(i):
                    take_turned(i)
                if has(i - 1):
                    store(i - 1, (j + 1) % 2)

            steps(act, step)
            for par in range(2):
                act.wait_ge(out_st[par], 16 * B // 2)

        @block.gpsimd
        def _(pool):
            pool.memset(bk[:, :], 0.0).then_inc(zero_k, 1)
            pool.wait_ge(su_pe, 5)
            pool.memset(bv[:, :], 0.0).then_inc(zero_v, 1)

            def v_parts(b):
                after(pool, v0_ready, b)
                pool.tensor_tensor(v3[:, 1, :], v3[:, 0, :], halves(v3[:, 0, :])[:, 1::2], ALU.subtract).then_inc(v1_ready, 1)
                after(pool, v1_ready, b)
                pool.tensor_tensor(v3[:, 2, :], v3[:, 1, :], halves(v3[:, 1, :])[:, 1::2], ALU.subtract).then_inc(v3_ready, 1)

            def some_values_to_diagonal(b):
                pool.wait_ge(zero_v, 1)
                after(pool, v3_ready, b)
                after(pool, av_done, b - 1)
                dst = bv[:, :].rearrange("p (w a t n) -> p w a t n", w=PARTS, a=2, t=G)
                src = v3[:, :, :].rearrange("p w (v n) -> p w v n", v=2)
                for to, at, a, v in VALUE_BLOCKS[0:ON_POOL]:
                    pool.dma_start(dst[to:to + 16, :, a, to // 16, :], src[at:at + 16, :, v, :]).then_inc(bv_pool, 16)

            def make_x2(b, slot):
                after(pool, yc_ready, b)
                after(pool, x1_ready, b)
                after(pool, x3_ready, b - UNROLL)
                after(pool, key_done, b - UNROLL)
                pool.tensor_tensor(x2[:, slot, :], x1[:, :], yc[:, :], ALU.add).then_inc(x2_ready, 1)

            def probs(b):
                after(pool, inv_ready, b)
                after(pool, ex_ready, b)
                after(pool, a0_ready, b - 1)
                pool.tensor_tensor(pr[:, :].rearrange("p (u j) -> p u j", j=H), ex[:, :].rearrange("p (u j) -> p u j", j=H),
                                   sinv[:, :].unsqueeze(2).to_broadcast([P, NU, H]), ALU.mult).then_inc(pr_ready, 1)

            def make_x3(b, slot):
                after(pool, z_ready, b)
                after(pool, x2_ready, b)
                after(pool, r_done, b - 1)
                after(pool, xo_ready, b - 1)
                pool.tensor_tensor(x3[:, :], x2[:, slot, :], zz[:, :], ALU.add).then_inc(x3_ready, 1)

            def step(i, j):
                if has(i - 1):
                    make_x3(i - 1, (j - 1) % UNROLL)
                if has(i + 3):
                    make_x2(i + 3, (j + 3) % UNROLL)
                if has(i + 1):
                    v_parts(i + 1)
                    probs(i + 1)
                    some_values_to_diagonal(i + 1)

            steps(pool, step)

        @block.vector
        def _(dve):
            count = [0]

            def setup(ins):
                count[0] += 1
                ins.then_inc(su_dve, 1)
                dve.wait_ge(su_dve, count[0])

            dve.wait_ge(su_pe, 1)
            styles = ps_h[:, 0:3 * C * B].rearrange("p (n c b) -> p n c b", n=3, c=C)
            for n in range(3):
                for c in range(C):
                    ins = dve.tensor_scalar(sty[:, n, c, :], styles[:, n, c, :], GAIN if n == 0 else 1.0,
                                            afb[:, n, c:c + 1], ALU.mult, ALU.add)
                setup(ins)
            assert count[0] == SU_STY
            setup(dve.tensor_copy(pa_all[:, :, PA_STYLE1:PA_STYLE1 + 2].rearrange("p b c -> p c b"), sty[:, 0, :, :]))
            setup(dve.tensor_tensor(sty2[:, :, :, :].rearrange("p n c b -> p (n c b)"), sty[:, :, :, :].rearrange("p n c b -> p (n c b)"),
                                    sty[:, :, :, :].rearrange("p n c b -> p (n c b)"), ALU.mult))
            assert count[0] == SU_STY2
            dve.tensor_copy(pa_all[:, :, PA_STYLEK:PA_STYLEK + 2].rearrange("p b c -> p c b"), sty[:, 1, :, :])
            dve.tensor_copy(pb_all[:, :, PB_STYLEO:PB_STYLEO + 2].rearrange("p b c -> p c b"), sty[:, 2, :, :])
            dve.wait_ge(su_pe, 3)
            dve.tensor_scalar(rk0[:, :], ps_g[0:B, 0, 0:D], EPS, None, ALU.add)
            setup(dve.tensor_scalar(dem[:, :, :, :].rearrange("p n c b -> p (n c b)"), ps_k[:, 0:2 * C * B], EPS, None, ALU.add))
            assert count[0] == SU_VAR
            dve.wait_ge(su_act, 2)
            flat = [t[:, :, :, :].rearrange("p n c b -> p (n c b)") for t in (dem, dt1, dt2)]

            def newton(var, root, tmp, out):
                yield dve.reciprocal(tmp, root)
                yield dve.tensor_tensor(root, tmp, tmp, ALU.mult)
                yield dve.tensor_tensor(root, root, var, ALU.mult)
                yield dve.tensor_scalar(root, root, -0.5, 1.5, ALU.mult, ALU.add)
                yield dve.tensor_tensor(out, root, tmp, ALU.mult)

            rkd = rows[:, R_DK:R_DK + D]
            dve.tensor_copy(rows[:, 0:2 * HID], ps_f[0:B, 0:2 * HID])
            dve.tensor_copy(rows[:, R_UG:R_UG + 2 * D], ps_1[0:B, :])
            for ins in newton(rk0[:, :], rk1[:, :], kx[0:B, 0, 0:D], rkd):
                setup(ins)
            assert count[0] == SU_ROWS
            for ins in newton(flat[0], flat[1], flat[2], flat[0]):
                setup(ins)
            dve.tensor_copy(pa_all[:, :, PA_DEMOD1:PA_DEMOD1 + 2].rearrange("p b c -> p c b"), dem[:, 0, :, :])
            dve.tensor_copy(pb_all[:, :, PB_DEMODO:PB_DEMODO + 2].rearrange("p b c -> p c b"), dem[:, 1, :, :])
            dve.wait_ge(su_pe, 4)
            banks = (ps_g[:, 1, :], ps_g[:, 2, :], ps_g[:, 3, :], ps_h[:, :])
            for c in range(C):
                for half in range(2):
                    k0, k1 = 16 * half, min(K, 16 * half + 16)
                    src = banks[2 * c + half][:, 0:(k1 - k0) * B].rearrange("p (k b) -> p k b", b=B)
                    dst = pb_all[:, :, PB_U + c * K + k0:PB_U + c * K + k1].rearrange("p b k -> p k b")
                    dve.tensor_tensor(dst, src, bds[:, c, k0:k1].unsqueeze(2).to_broadcast([P, k1 - k0, B]), ALU.add)
            setup(dve.memset(pb_all[:, :, PB_ULAST:PB_ULAST + 1], 0.0))
            dve.wait_ge(su_pe, 5)
            setup(dve.tensor_scalar(pb_all[0:K, :, PB_ULAST], ps_k[0:K, 0:B], bdl[:, 0:1], None, ALU.add))
            assert count[0] == SU_U

            def make_weights(b, par):
                dve.wait_ge(bc_in[par], pair_count(b, par))
                row = bc[:, par, :]
                after(dve, down_done, b - 1)
                both = [P, C, HID]
                dve.tensor_tensor(wd[:, :, :], dpj[:, :, :], row[:, R_DG:R_DG + HID].unsqueeze(1).to_broadcast(both),
                                  ALU.mult).then_inc(wd_half, 1)
                after(dve, up_done, b - 1)
                dve.tensor_tensor(wu[:, :], upj[:, :], row[0:HID, R_UG:R_UG + D], ALU.mult).then_inc(wu_half, 1)
                after(dve, wd_half, b)
                dve.tensor_tensor(wd[:, :, :], wd[:, :, :], row[:, R_DB:R_DB + HID].unsqueeze(1).to_broadcast(both),
                                  ALU.add).then_inc(wd_ready, 1)
                after(dve, wu_half, b)
                dve.tensor_tensor(wu[:, :], wu[:, :], row[0:HID, R_UB:R_UB + D], ALU.add).then_inc(wu_ready, 1)

            def make_wk(b, par):
                after(dve, pa_ready, b)
                after(dve, key_done, b - 1)
                for c in range(C):
                    ins = dve.scalar_tensor_tensor(out=wk[:, c, :], in0=wks[:, c, :], scalar=pa[:, PA_STYLEK + c:PA_STYLEK + c + 1],
                                                   in1=bc[:, par, R_DK:R_DK + D], op0=ALU.mult, op1=ALU.mult)
                ins.then_inc(wk_ready, 1)

            def make_x1(b, par):
                after(dve, up_done, b)
                after(dve, l1_done, b - 1)
                after(dve, x2_ready, b - 1)
                dve.scalar_tensor_tensor(out=x1[:, :], in0=xin[:, par, :], scalar=2.0, in1=ps_f[:, :],
                                         op0=ALU.mult, op1=ALU.add).then_inc(x1_ready, 1)

            def clip(b):
                after(dve, y1_ready, b)
                after(dve, x2_ready, b - 1)
                dve.tensor_scalar(yc[:, :], y1[:, :], -CLAMP, CLAMP, ALU.max, ALU.min).then_inc(yc_ready, 1)

            def take_keys(b, slot):
                after(dve, key_done, b)
                after(dve, v0_ready, b - 2)
                dve.tensor_tensor(kx[:, slot, :].rearrange("p (a n) -> p a n", a=2), ps_k[:, :].rearrange("p (a n) -> p a n", a=2),
                                  kbs[:, :].unsqueeze(1).to_broadcast([P, 2, D]), ALU.add).then_inc(kx_ready, 1)

            def keys(b, slot):
                after(dve, kx_ready, b)
                after(dve, s_done, b - 2)
                parts = k3[:, slot, :, :]
                dve.transpose(parts[:, 0, :], kx[:, slot, :].rearrange("p (a h d) -> p h a d", a=2, h=H)).then_inc(k0_ready, 1)
                after(dve, k0_ready, b)
                dve.tensor_tensor(parts[:, 1, :], parts[:, 0, :], halves(parts[:, 0, :])[:, 1::2], ALU.subtract).then_inc(k1_ready, 1)
                after(dve, k1_ready, b)
                dve.tensor_tensor(parts[:, 2, :], parts[:, 1, :], halves(parts[:, 1, :])[:, 1::2], ALU.subtract).then_inc(k3_ready, 1)

            def turn_values(b, slot):
                after(dve, kx_ready, b)
                after(dve, bv_in, b - 1, 16 * (16 - ON_POOL))
                after(dve, bv_pool, b - 1, 16 * ON_POOL)
                dve.transpose(v3[:, 0, :].rearrange("p (v d g) -> p d v g", v=2, d=DH),
                              kx[:, slot, :].rearrange("p (a j d) -> p d a j", a=2, j=H)).then_inc(v0_ready, 1)

            def add_magnitudes(out, lo_ready, mid_ready, ready, b):
                out = out[:, :].rearrange("p (b u h) -> p b u h", b=NU // PER_BANK, u=PER_BANK)
                after(dve, lo_ready, b)
                dve.tensor_tensor(out, magnitude[:, 1], out, ALU.add).then_inc(mid_ready, 1)
                after(dve, mid_ready, b)
                dve.tensor_tensor(out, magnitude[:, 0], out, ALU.add).then_inc(ready, 1)

            def softmax_shift(b):
                add_magnitudes(sc, slo_ready, smid_ready, sc_ready, b)
                after(dve, sc_ready, b)
                scores = sc[:, :].rearrange("p (u j) -> p u j", j=H)
                dve.tensor_reduce(smax[:, :], scores, AX.X, ALU.max).then_inc(max_ready, 1)
                after(dve, max_ready, b)
                dve.tensor_tensor(scores, scores, smax[:, :].unsqueeze(2).to_broadcast([P, NU, H]), ALU.subtract).then_inc(sd_ready, 1)

            def softmax_sum(b):
                after(dve, ex_ready, b)
                dve.tensor_reduce(ssum[:, :], ex[:, :].rearrange("p (u j) -> p u j", j=H), AX.X, ALU.add).then_inc(sum_ready, 1)
                after(dve, sum_ready, b)
                after(dve, pr_ready, b - 1)
                dve.reciprocal(sinv[:, :], ssum[:, :]).then_inc(inv_ready, 1)

            def prob_parts(b):
                after(dve, pr_ready, b)
                after(dve, av_done, b - 1)
                dve.transpose(a3[:, 0, :], pr[:, :].rearrange("p (v g j) -> p g v j", v=2, j=H)).then_inc(a0_ready, 1)
                after(dve, a0_ready, b)
                dve.tensor_tensor(a3[:, 1, :], a3[:, 0, :], halves(a3[:, 0, :])[:, 1::2], ALU.subtract).then_inc(a1_ready, 1)
                after(dve, a1_ready, b)
                dve.tensor_tensor(a3[:, 2, :], a3[:, 1, :], halves(a3[:, 1, :])[:, 1::2], ALU.subtract).then_inc(a3_ready, 1)

            def turn_attended(b):
                after(dve, av_ready, b)
                after(dve, t_done, b - 1)
                dve.transpose(on[:, :].rearrange("p (v h d) -> p h v d", v=2, h=H),
                              av[:, :].rearrange("p (g a h) -> p h a g", a=2, h=H)).then_inc(on_ready, 1)

            def make_out(b, par):
                after(dve, l3_done, b)
                after(dve, x3_ready, b)
                if not isinstance(b, int) or b >= 2:
                    dve.wait_ge(out_st[par], (b - par) * 8)
                dve.tensor_tensor(xo[:, par, :], x3[:, :], ps_f[:, :], ALU.add).then_inc(xo_ready, 1)

            def step(i, j):
                if has(i + 3):
                    make_wk(i + 3, (j + 1) % 2)
                if has(i + 1):
                    softmax_shift(i + 1)
                if has(i + 3):
                    clip(i + 3)
                if has(i + 1):
                    softmax_sum(i + 1)
                    turn_values(i + 1, (j + 1) % 2)
                if has(i + 4):
                    make_weights(i + 4, j % 2)
                if has(i):
                    add_magnitudes(av, alo_ready, amid_ready, av_ready, i)
                if has(i + 3):
                    take_keys(i + 3, (j + 1) % 2)
                if has(i):
                    turn_attended(i)
                if has(i - 1):
                    make_out(i - 1, (j + 1) % 2)
                if has(i + 3):
                    keys(i + 3, (j + 1) % 2)
                if has(i + 4):
                    make_x1(i + 4, j % 2)
                if has(i + 1):
                    prob_parts(i + 1)

            steps(dve, step)


def kernel(x, cond_512, L0_cond_down_project, L0_cond_down_gamma, L0_cond_down_beta, L0_cond_up_project,
           L0_cond_up_gamma, L0_cond_up_beta, L1_cond_weight, L1_cond_bias, L1_cond_affine_w, L1_cond_affine_b,
           L2_cond_k_aff_w, L2_cond_k_aff_b, L2_cond_k_w, L2_cond_k_b, L2_cond_o_aff_w, L2_cond_o_aff_b,
           L2_cond_o_w, L2_cond_o_b, L3_cond_W_dec, L3_cond_b_dec, L3_cond_V):
    import numpy as _np
    import concourse.bacc as _bacc
    from concourse import mybir as _mybir
    from concourse.bass_utils import run_bass_kernel_spmd as _run

    B, S, D = x.shape
    K = L3_cond_V.shape[0]

    def chunks(w):
        w = _np.asarray(w)
        return w.reshape(D // 128, 128, -1).transpose(1, 0, 2)

    def column(v):
        return _np.asarray(v).reshape(D // 128, 128).T

    arrays = {
        "xT": _np.asarray(x).transpose(0, 2, 1).reshape(B, D // 128, 128, S).transpose(0, 2, 1, 3),
        "condT": _np.asarray(cond_512).T,
        "gb_down": _np.concatenate([_np.asarray(L0_cond_down_gamma), _np.asarray(L0_cond_down_beta)], 1),
        "gb_up": _np.concatenate([_np.asarray(L0_cond_up_gamma), _np.asarray(L0_cond_up_beta)], 1),
        "dproj": chunks(L0_cond_down_project),
        "uproj": _np.asarray(L0_cond_up_project),
        "w1T": chunks(_np.asarray(L1_cond_weight).T),
        "bias1": column(L1_cond_bias),
        "aff1T": _np.asarray(L1_cond_affine_w).T,
        "affb1": column(L1_cond_affine_b),
        "wkT": chunks(_np.asarray(L2_cond_k_w).T),
        "affkT": _np.asarray(L2_cond_k_aff_w).T,
        "affbk": column(L2_cond_k_aff_b),
        "kb": _np.asarray(L2_cond_k_b).reshape(1, D),
        "woT": chunks(_np.asarray(L2_cond_o_w).T),
        "affoT": _np.asarray(L2_cond_o_aff_w).T,
        "affbo": column(L2_cond_o_aff_b),
        "ob": column(L2_cond_o_b),
        "wdec": _np.asarray(L3_cond_W_dec),
        "bdec": chunks(_np.asarray(L3_cond_b_dec)[:D * K].reshape(D, K)),
        "bdec_last": _np.asarray(L3_cond_b_dec)[D * K:].reshape(K, 1),
        "vmat": _np.asarray(L3_cond_V),
        "ident": _np.eye(128, dtype=_np.float32),
    }
    arrays = {n: _np.ascontiguousarray(a) for n, a in arrays.items()}
    nc = _bacc.Bacc("TRN2", target_bir_lowering=False, num_devices=1)
    args = [nc.dram_tensor(n, a.shape, _mybir.dt.from_np(a.dtype), kind="ExternalInput").ap() for n, a in arrays.items()]
    args.append(nc.dram_tensor("outT", arrays["xT"].shape, _mybir.dt.float32, kind="ExternalOutput").ap())
    build(nc, *args)
    r = _run(nc, [arrays], core_ids=[0])
    out = _np.asarray(r.results[0]["outT"])
    return out.transpose(0, 2, 1, 3).reshape(B, D, S).transpose(0, 2, 1)
```

```python
from contextlib import ExitStack

import numpy as np

import concourse.bass as bass
from concourse import mybir

F32 = mybir.dt.float32
BF16 = mybir.dt.bfloat16
ALU = mybir.AluOpType
ACT = mybir.ActivationFunctionType
AX = mybir.AxisListType

P = 128
C = 2
H, DH = 16, 16
G = 8
NU = 32
CLAMP = 256.0
EPS = 1e-8
PARTS = 3
BIAS_ROWS = 32 * PARTS
UNROLL = 4
PER_BANK = 8

PA_STYLE1, PA_STYLEK, PA_DEMOD1, PA_N = 0, 2, 4, 6
PB_STYLEO, PB_DEMODO, PB_ULAST, PB_U = 0, 2, 4, 5


def build(nc, xT, condT, from_cond, w3T, columns, dproj, uproj, kb, wdec, bdec, bdec_last, vmat, ident, outT):
    B, _, _, S = xT.shape
    D = C * P
    HID = uproj.shape[0]
    K = vmat.shape[0]
    CD = condT.shape[0]
    GAIN = float(np.float32(1.0) / np.sqrt(CD).astype(np.float32))
    SCALE = 1.0 / float(np.sqrt(DH))
    PB_N = PB_U + C * K
    NROW = 2 * HID + 2 * D + D
    R_DG, R_DB, R_UG, R_UB, R_DK = 0, HID, 2 * HID, 2 * HID + D, 2 * HID + 2 * D
    W = C * S
    assert W == 512 and S == 2 * P and D == H * DH

    with ExitStack() as ctx:
        def sb(name, shape, dt=F32):
            return ctx.enter_context(nc.sbuf_tensor(name, shape, dt))

        def psum(name):
            return ctx.enter_context(nc.psum_tensor(name, [P, W], F32))

        def sem(name):
            return ctx.enter_context(nc.semaphore(name))

        rows_dram = nc.dram_tensor("rows_dram", [B, NROW], F32).ap()

        cond = sb("cond", [CD, B])
        dpj, upj = sb("dpj", [P, C, HID]), sb("upj", [HID, D])
        w3s = sb("w3s", [P, 3, C, D])
        w1s, wks, wos = (w3s[:, n] for n in range(3))
        cols = sb("cols", [P, 5, C])
        afb, b1s, obs = cols[:, 0:3], cols[:, 3], cols[:, 4]
        kb3 = sb("kb3", [BIAS_ROWS, D])
        pick = sb("pick", [BIAS_ROWS, P], BF16)
        bds, bdl = sb("bds", [P, C, K]), sb("bdl", [K, 1])
        vms = sb("vms", [K, D])
        idn = sb("idn", [P, P])
        pa_all, pb_all = sb("pa_all", [P, B, PA_N]), sb("pb_all", [P, B, PB_N])
        bc = sb("bc", [P, 2, NROW])
        pa, pb = sb("pa", [P, PA_N]), sb("pb", [P, PB_N])
        wd, wu = sb("wd", [P, C, HID]), sb("wu", [HID, D])
        w1, wk, wo = sb("w1", [P, C, D]), sb("wk", [P, C, D]), sb("wo", [P, C, D])
        xin = sb("xin", [P, 2, W])
        hid = sb("hid", [HID, S])
        x1, y1, yc = sb("x1", [P, W]), sb("y1", [P, W]), sb("yc", [P, W])
        x2 = sb("x2", [P, UNROLL, W])
        kx = sb("kx", [P, 2, W])
        k3 = sb("k3", [P, 2, PARTS, W])
        v3, a3 = sb("v3", [P, 2, PARTS, W]), sb("a3", [P, PARTS, W])
        bk, bv = sb("bk", [P, PARTS * G * W]), sb("bv", [P, PARTS * G * W])
        smax, ssum, sinv = sb("smax", [P, NU]), sb("ssum", [P, NU]), sb("sinv", [P, NU])
        sc, ex, pr = sb("sc", [P, W]), sb("ex", [P, W]), sb("pr", [P, W])
        av, on, ot = sb("av", [P, W]), sb("on", [P, W]), sb("ot", [P, W])
        zz, x3 = sb("zz", [P, W]), sb("x3", [P, W])
        rr = sb("rr", [K, S])
        xo = sb("xo", [P, 2, W])
        at = (D + 1) * K
        wds = bv[:, 0:at]
        fcs = bv[0:CD, at:at + 5 * D + 2 * HID]
        afs = [fcs[:, n * D:(n + 1) * D] for n in range(3)]
        at += 5 * D + 2 * HID
        rows = bv[0:B, at:at + NROW]
        at += NROW
        rk0, rk1 = bv[0:B, at:at + D], bv[0:B, at + D:at + 2 * D]
        at += 2 * D

        def setup_columns(at, n):
            return bv[:, at:at + n * C * B].rearrange("p (n c b) -> p n c b", n=n, c=C)

        sty, sty2 = setup_columns(at, 3), setup_columns(at + 3 * C * B, 3)
        at += 6 * C * B
        dem, dt1, dt2 = (setup_columns(at + 2 * C * B * n, 2) for n in range(3))
        assert at + 6 * C * B <= PARTS * G * W
        gbd, gbu = fcs[:, 3 * D:3 * D + 2 * HID], fcs[:, 3 * D + 2 * HID:]

        ps_h, ps_f, ps_1, ps_k = (psum(n) for n in ("ps_h", "ps_f", "ps_1", "ps_k"))
        ps_t, ps_o = ps_1, ps_k
        ps_g = ctx.enter_context(nc.psum_tensor("ps_g", [P, NU // PER_BANK, W], F32))
        magnitude = ps_g[:, :, 0:PER_BANK * PARTS * H].rearrange("p b (u m h) -> p m b u h", u=PER_BANK, m=PARTS)

        ld_cond, ld_w3, ld_small = sem("ld_cond"), sem("ld_w3"), sem("ld_small")
        ld_wdec = sem("ld_wdec")
        rows_out = sem("rows_out")
        x_in = [sem("x_in0"), sem("x_in1")]
        bc_in = [sem("bc_in0"), sem("bc_in1")]
        out_st = [sem("out_st0"), sem("out_st1")]
        bk_in, bv_in = sem("bk_in"), sem("bv_in")
        bv_pool = sem("bv_pool")
        zero_k, zero_v, pick_ready = sem("zero_k"), sem("zero_v"), sem("pick_ready")
        su_pe, su_act, su_dve = sem("su_pe"), sem("su_act"), sem("su_dve")
        dec_done, dec_turned, dec_out = sem("dec_done"), sem("dec_turned"), sem("dec_out")
        kb_ready = sem("kb_ready")
        pa_ready, pb_ready, w1_ready, wo_ready = sem("pa_ready"), sem("pb_ready"), sem("w1_ready"), sem("wo_ready")
        wd_half, wu_half = sem("wd_half"), sem("wu_half")
        wd_ready, wu_ready, wk_ready = sem("wd_ready"), sem("wu_ready"), sem("wk_ready")
        down_done, up_done, l1_done, key_done = sem("down_done"), sem("up_done"), sem("l1_done"), sem("key_done")
        hid_ready, x1_ready, y1_ready, yc_ready, x2_ready = (
            sem("hid_ready"), sem("x1_ready"), sem("y1_ready"), sem("yc_ready"), sem("x2_ready"))
        kx_ready, k0_ready, k1_ready, k3_ready = sem("kx_ready"), sem("k0_ready"), sem("k1_ready"), sem("k3_ready")
        v0_ready, v1_ready, v3_ready = sem("v0_ready"), sem("v1_ready"), sem("v3_ready")
        s_done, max_ready, sd_ready, ex_ready = sem("s_done"), sem("max_ready"), sem("sd_ready"), sem("ex_ready")
        slo_ready, smid_ready, sc_ready = sem("slo_ready"), sem("smid_ready"), sem("sc_ready")
        alo_ready, amid_ready, av_ready = sem("alo_ready"), sem("amid_ready"), sem("av_ready")
        sum_ready, inv_ready, pr_ready = sem("sum_ready"), sem("inv_ready"), sem("pr_ready")
        a0_ready, a1_ready, a3_ready = sem("a0_ready"), sem("a1_ready"), sem("a3_ready")
        av_done, on_ready, t_done, ot_ready = sem("av_done"), sem("on_ready"), sem("t_done"), sem("ot_ready")
        o_done, z_ready, x3_ready = sem("o_done"), sem("z_ready"), sem("x3_ready")
        r_done, rr_ready, l3_done, xo_ready = sem("r_done"), sem("rr_ready"), sem("l3_done"), sem("xo_ready")

        def after(eng, s, b, per=1):
            if isinstance(b, int) and b < 0:
                return
            eng.wait_ge(s, (b + 1) * per if per > 1 else b + 1)

        def pair_count(b, par):
            return (b - par) * 8 + 16

        VALUE_BLOCKS = [(32 * q + 16 * v, 32 * q + 16 * a, a, v) for q in range(4) for v in range(2) for a in range(2)]
        ON_POOL = 5

        def halves(t):
            return t.bitcast(BF16)

        N_SMALL = 7
        SU_STY, SU_STY2, SU_VAR, SU_ROWS, SU_PARAMS = 3, 5, 6, 11, 19
        FIRST, LAST = 3, 27
        assert (LAST - FIRST) % UNROLL == 0 and LAST + 4 < B

        def has(b):
            return not isinstance(b, int) or 0 <= b < B

        def steps(eng, step, early=None):
            for i in range(-4, FIRST):
                if early is not None:
                    early(i)
                step(i, i % UNROLL)
            with eng.Fori(FIRST, LAST - UNROLL + 1, UNROLL) as i:
                for j in range(UNROLL):
                    step(i + j, (FIRST + j) % UNROLL)
            for i in range(LAST, B + 1):
                step(i, i % UNROLL)

        block = ctx.enter_context(nc.Block())

        @block.sync
        def _(sp):
            sp.dma_start(cond[:, :], condT).then_inc(ld_cond, 16)
            sp.dma_start(fcs, from_cond).then_inc(ld_cond, 16)
            sp.dma_start(cols[:, :, :], columns).then_inc(ld_cond, 16)
            sp.dma_start(w3s[:, :, :, :], w3T).then_inc(ld_w3, 16)
            small = [(dpj[:, :, :], dproj), (upj[:, :], uproj), (kb3[:, :], kb.to_broadcast([BIAS_ROWS, D])),
                     (bds[:, :, :], bdec), (bdl[:, :], bdec_last), (vms[:, :], vmat), (idn[:, :], ident)]
            assert len(small) == N_SMALL
            for dst, src in small:
                sp.dma_start(dst, src).then_inc(ld_small, 16)
            sp.dma_start(wds, wdec).then_inc(ld_wdec, 16)
            sp.dma_start(xin[:, 0, :], xT[0].rearrange("p c s -> p (c s)")).then_inc(x_in[0], 16)
            sp.dma_start(xin[:, 1, :], xT[1].rearrange("p c s -> p (c s)")).then_inc(x_in[1], 16)
            sp.wait_ge(su_dve, SU_ROWS)
            sp.dma_start(rows_dram, rows[:, :]).then_inc(rows_out, 16)
            sp.wait_ge(rows_out, 16)
            for b in range(2):
                sp.dma_start(bc[:, b, :], rows_dram[b:b + 1, :].to_broadcast([P, NROW])).then_inc(bc_in[b], 16)

            def keys_to_diagonal(b, slot):
                after(sp, k3_ready, b)
                after(sp, s_done, b - 1)
                dst = bk[:, :].rearrange("p (w t n) -> p w t n", w=PARTS, t=G)
                for t in range(G):
                    sp.dma_start(dst[16 * t:16 * t + 16, :, t, :], k3[16 * t:16 * t + 16, slot, :, :]).then_inc(bk_in, 16)

            def values_to_diagonal(b, slot):
                after(sp, av_done, b - 1)
                after(sp, v3_ready, b)
                dst = bv[:, :].rearrange("p (w a t n) -> p w a t n", w=PARTS, a=2, t=G)
                src = v3[:, slot, :, :].rearrange("p w (v n) -> p w v n", v=2)
                for to, at, a, v in VALUE_BLOCKS[ON_POOL:]:
                    sp.dma_start(dst[to:to + 16, :, a, to // 16, :], src[at:at + 16, :, v, :]).then_inc(bv_in, 16)

            sp.wait_ge(zero_k, 1)
            keys_to_diagonal(0, 0)
            keys_to_diagonal(1, 1)
            sp.wait_ge(zero_v, 1)
            values_to_diagonal(0, 0)
            with sp.Fori(2, B - 1, 2) as b:
                keys_to_diagonal(b, 0)
                values_to_diagonal(b - 1, 1)
                keys_to_diagonal(b + 1, 1)
                values_to_diagonal(b, 0)
            values_to_diagonal(B - 1, 1)

        @block.tensor
        def _(pe):
            pe.wait_ge(ld_cond, 16 * 3)
            for n in range(3):
                for c in range(C):
                    mm = pe.matmul(ps_h[:, (n * C + c) * B:(n * C + c + 1) * B], afs[n][:, c * P:(c + 1) * P],
                                   cond[:, :], start=True, stop=True, skip_group_check=True)
            mm.then_inc(su_pe, 1)
            pe.matmul(ps_f[0:B, 0:2 * HID], cond[:, :], gbd, start=True, stop=True)
            pe.matmul(ps_1[0:B, :], cond[:, :], gbu, start=True, stop=True).then_inc(su_pe, 1)
            pe.wait_ge(su_act, 1)
            pe.wait_ge(su_dve, SU_STY2)
            for n, sq in ((0, x2[:, 0, :]), (1, x2[:, 1, :])):
                for o in range(C):
                    for c in range(C):
                        mm = pe.matmul(ps_k[:, (n * C + o) * B:(n * C + o + 1) * B],
                                       sq[:, c * D + o * P:c * D + (o + 1) * P], sty2[:, 2 * n, c, :],
                                       start=(c == 0), stop=(c == C - 1), skip_group_check=True)
            for c in range(C):
                mm = pe.matmul(ps_g[0:B, 0, 0:D], sty2[:, 1, c, :], x3[:, c * D:(c + 1) * D],
                               start=(c == 0), stop=(c == C - 1))
            mm.then_inc(su_pe, 1)
            pe.wait_ge(ld_small, 16 * N_SMALL)
            pe.wait_ge(ld_wdec, 16)
            pe.wait_ge(su_dve, SU_VAR)
            pe.matmul(ps_k[0:K, 0:B], wds[:, D * K:(D + 1) * K], cond[:, :], start=True, stop=True).then_inc(su_pe, 1)
            def decoder(part):
                c, k0 = part // 2, (part % 2) * (K // 2)
                of_feature = wds[:, c * P * K:(c + 1) * P * K].rearrange("p (q f k) -> p q k f", q=4, k=K)
                for q in range(4):
                    mm = pe.matmul(ps_g[32 * q:32 * q + 32, part, 0:K // 2 * 32], cond[:, :],
                                   of_feature[:, q, k0:k0 + K // 2, :], start=True, stop=True, skip_group_check=True)
                mm.then_inc(dec_done, 1)

            def early(i):
                if i == -4:
                    for part in range(4):
                        decoder(part)
                    pe.wait_ge(su_dve, SU_PARAMS)
                if i == -3:
                    pe.wait_ge(kb_ready, 1)
                    pe.wait_ge(pick_ready, 1 + PARTS)
                if i == -1:
                    pe.wait_ge(dec_turned, 4)

            def last_row(b):
                return min(b, B - 1) if isinstance(b, int) else b

            def down(b, par):
                after(pe, wd_ready, b)
                pe.wait_ge(x_in[par], pair_count(b, par))
                after(pe, hid_ready, b - 1)
                after(pe, rr_ready, b - 5)
                for c in range(C):
                    mm = pe.matmul(ps_h[0:HID, 0:S], wd[:, c, :], xin[:, par, c * S:(c + 1) * S],
                                   start=(c == 0), stop=(c == C - 1))
                mm.then_inc(down_done, 1)

            def up(b):
                after(pe, wu_ready, b)
                after(pe, hid_ready, b)
                after(pe, x1_ready, b - 1)
                after(pe, xo_ready, b - 5)
                for c in range(C):
                    mm = pe.matmul(ps_f[:, c * S:(c + 1) * S], wu[:, c * P:(c + 1) * P], hid[:, :],
                                   start=True, stop=True, skip_group_check=True)
                mm.then_inc(up_done, 1)

            def l1(b):
                after(pe, w1_ready, b)
                after(pe, x1_ready, b)
                after(pe, y1_ready, b - 1)
                after(pe, ot_ready, b - 4)
                for o in range(C):
                    for c in range(C):
                        mm = pe.matmul(ps_1[:, o * S:(o + 1) * S], w1[:, c, o * P:(o + 1) * P],
                                       x1[:, c * S:(c + 1) * S], start=(c == 0), stop=(c == C - 1),
                                       skip_group_check=True)
                mm.then_inc(l1_done, 1)

            def key(b, slot):
                after(pe, wk_ready, b)
                after(pe, x2_ready, b)
                after(pe, kx_ready, b - 1)
                after(pe, z_ready, b - 4)
                for a in range(2):
                    pe.matmul(ps_k[:, a * D:(a + 1) * D], pick[:, :], halves(kb3[:, :])[:, 1::2],
                              start=True, stop=False, skip_group_check=True)
                    for c in range(C):
                        mm = pe.matmul(ps_k[:, a * D:(a + 1) * D], x2[:, slot, c * S + a * P:c * S + (a + 1) * P],
                                       wk[:, c, :], start=False, stop=(c == C - 1), skip_group_check=True)
                mm.then_inc(key_done, 1)

            def grouped(g, diag, at, col_step, rows3, row_at, row_step):
                diag, rows3 = halves(diag), halves(rows3)
                for w in range(PARTS):
                    lo = 2 * (w * G * W + at) + 1
                    moving = rows3[:, 0:PARTS - w, 2 * row_at + 1:2 * (row_at + row_step * (H - 1)) + 2:2 * row_step]
                    out = ps_g[:, g // PER_BANK, (g % PER_BANK) * PARTS * H + w * H:(g % PER_BANK + 1) * PARTS * H]
                    mm = pe.matmul(out, diag[:, lo:lo + 2 * col_step * (P - 1) + 1:2 * col_step], moving,
                                   start=(g % PER_BANK == 0 and w == 0), stop=(g % PER_BANK == PER_BANK - 1 and w == PARTS - 1),
                                   skip_group_check=True)
                return mm

            def scores(b, slot):
                after(pe, bk_in, b, 16 * G)
                after(pe, k3_ready, b)
                after(pe, av_ready, b - 2)
                for u in range(NU):
                    mm = grouped(u, bk[:, :], u, NU, k3[:, slot, :, :], u, NU)
                mm.then_inc(s_done, 1)

            def attend(b):
                after(pe, bv_in, b, 16 * (16 - ON_POOL))
                after(pe, bv_pool, b, 16 * ON_POOL)
                after(pe, a3_ready, b)
                after(pe, sc_ready, last_row(b + 1))
                for g in range(NU):
                    mm = grouped(g, bv[:, :], (g % 2) * G * W // 2 + g // 2, H, a3[:, :, :], g * H, 1)
                mm.then_inc(av_done, 1)

            def turn(b):
                after(pe, on_ready, b)
                after(pe, ot_ready, b - 1)
                after(pe, y1_ready, last_row(b + 3))
                for c in range(C):
                    dst = ps_t[:, c * S:(c + 1) * S].rearrange("p (a q v g) -> p v q a g", a=2, q=4, v=2)
                    for v in range(2):
                        mm = pe.transpose(dst[:, v], on[:, v * D + c * P:v * D + (c + 1) * P], idn[:, :])
                mm.then_inc(t_done, 1)

            def out_proj(b):
                after(pe, wo_ready, b)
                after(pe, ot_ready, b)
                after(pe, z_ready, b - 1)
                after(pe, kx_ready, last_row(b + 3))
                for o in range(C):
                    for c in range(C):
                        mm = pe.matmul(ps_o[:, o * S:(o + 1) * S], wo[:, c, o * P:(o + 1) * P],
                                       ot[:, c * S:(c + 1) * S], start=(c == 0), stop=(c == C - 1),
                                       skip_group_check=True)
                mm.then_inc(o_done, 1)

            def l3_in(b):
                after(pe, pb_ready, b)
                after(pe, x3_ready, b)
                after(pe, hid_ready, last_row(b + 4))
                after(pe, rr_ready, b - 1)
                for c in range(C):
                    mm = pe.matmul(ps_h[0:K, 0:S], pb[:, PB_U + c * K:PB_U + (c + 1) * K],
                                   x3[:, c * S:(c + 1) * S], start=(c == 0), stop=(c == C - 1))
                mm.then_inc(r_done, 1)

            def l3_out(b):
                after(pe, rr_ready, b)
                after(pe, x1_ready, last_row(b + 4))
                after(pe, xo_ready, b - 1)
                for c in range(C):
                    mm = pe.matmul(ps_f[:, c * S:(c + 1) * S], vms[:, c * P:(c + 1) * P], rr[:, :],
                                   start=True, stop=True, skip_group_check=True)
                mm.then_inc(l3_done, 1)

            def step(i, j):
                if has(i + 1):
                    scores(i + 1, (j + 1) % 2)
                if has(i + 3):
                    up(i + 3)
                if has(i - 1):
                    out_proj(i - 1)
                if has(i + 3):
                    l1(i + 3)
                if has(i):
                    attend(i)
                if has(i - 1):
                    l3_in(i - 1)
                if has(i + 3):
                    key(i + 3, (j + 3) % UNROLL)
                if has(i - 1):
                    l3_out(i - 1)
                if has(i + 4):
                    down(i + 4, j % 2)
                if has(i):
                    turn(i)

            steps(pe, step, early)

        @block.scalar
        def _(act):
            act.wait_ge(ld_w3, 16)
            act.activation(x2[:, 0, :], w1s[:, :, :].rearrange("p c d -> p (c d)"), ACT.Square)
            act.activation(x2[:, 1, :], wos[:, :, :].rearrange("p c d -> p (c d)"), ACT.Square)
            act.activation(x3[:, :], wks[:, :, :].rearrange("p c d -> p (c d)"), ACT.Square).then_inc(su_act, 1)
            act.wait_ge(su_dve, SU_VAR)
            act.activation(dt1[:, :, :, :], dem[:, :, :, :], ACT.Sqrt)
            act.activation(rk1[:, :], rk0[:, :], ACT.Sqrt).then_inc(su_act, 1)
            act.wait_ge(su_dve, SU_PARAMS)

            def load_x(b, par):
                after(act, x1_ready, b - 2)
                act.dma_start(xin[:, par, :], xT[bass.ds(b, 1), :, :, :].rearrange("o p c s -> p (o c s)")).then_inc(x_in[par], 16)

            def load_bc(b, par):
                after(act, wk_ready, b - 2)
                after(act, wd_ready, b - 2)
                after(act, wu_ready, b - 2)
                act.dma_start(bc[:, par, :], rows_dram[bass.ds(b, 1), :].to_broadcast([P, NROW])).then_inc(bc_in[par], 16)

            def store(b, par):
                after(act, xo_ready, b)
                act.dma_start(outT[bass.ds(b, 1), :, :, :].rearrange("o p c s -> p (o c s)"), xo[:, par, :]).then_inc(out_st[par], 16)

            def make_w1(b):
                after(act, wk_ready, b - 1)
                after(act, y1_ready, b - 1)
                act.copy(pa[:, :], pa_all[:, bass.ds(b, 1), :].rearrange("p o n -> p (o n)")).then_inc(pa_ready, 1)
                after(act, pa_ready, b)
                after(act, l1_done, b - 1)
                for c in range(C):
                    ins = act.activation(w1[:, c, :], w1s[:, c, :], ACT.Copy, scale=pa[:, PA_STYLE1 + c:PA_STYLE1 + c + 1])
                ins.then_inc(w1_ready, 1)

            def make_wo(b):
                after(act, r_done, b - 1)
                after(act, rr_ready, b - 1)
                act.copy(pb[:, :], pb_all[:, bass.ds(b, 1), :].rearrange("p o n -> p (o n)")).then_inc(pb_ready, 1)
                after(act, pb_ready, b)
                after(act, o_done, b - 1)
                for c in range(C):
                    ins = act.activation(wo[:, c, :], wos[:, c, :], ACT.Copy, scale=pb[:, PB_STYLEO + c:PB_STYLEO + c + 1])
                ins.then_inc(wo_ready, 1)

            def take_keys(b, slot):
                after(act, key_done, b)
                after(act, v0_ready, b - 2)
                act.copy(kx[:, slot, :], ps_k[:, :]).then_inc(kx_ready, 1)

            def relu(b):
                after(act, down_done, b)
                after(act, up_done, b - 1)
                act.activation(hid[:, :], ps_h[0:HID, 0:S], ACT.Relu).then_inc(hid_ready, 1)

            def y(b):
                after(act, l1_done, b)
                after(act, pa_ready, b)
                after(act, yc_ready, b - 1)
                for c in range(C):
                    ins = act.activation(y1[:, c * S:(c + 1) * S], ps_1[:, c * S:(c + 1) * S], ACT.Identity,
                                         scale=pa[:, PA_DEMOD1 + c:PA_DEMOD1 + c + 1], bias=b1s[:, c:c + 1])
                ins.then_inc(y1_ready, 1)

            def least(out, done, ready, b):
                after(act, done, b)
                act.copy(out[:, :].rearrange("p (b u h) -> p b u h", b=NU // PER_BANK, u=PER_BANK),
                         magnitude[:, PARTS - 1]).then_inc(ready, 1)

            def least_scores(b):
                after(act, ex_ready, b - 1)
                least(sc, s_done, slo_ready, b)

            def least_attended(b):
                after(act, on_ready, b - 1)
                least(av, av_done, alo_ready, b)

            def exp(b):
                after(act, sd_ready, b)
                after(act, pr_ready, b - 1)
                after(act, sum_ready, b - 1)
                act.activation(ex[:, :], sc[:, :], ACT.Exp, scale=SCALE).then_inc(ex_ready, 1)

            def take_turned(b):
                after(act, t_done, b)
                after(act, o_done, b - 1)
                act.copy(ot[:, :], ps_t[:, :]).then_inc(ot_ready, 1)

            def z(b):
                after(act, o_done, b)
                after(act, x3_ready, b - 1)
                for c in range(C):
                    ins = act.activation(zz[:, c * S:(c + 1) * S], ps_o[:, c * S:(c + 1) * S], ACT.Identity,
                                         scale=pb[:, PB_DEMODO + c:PB_DEMODO + c + 1], bias=obs[:, c:c + 1])
                ins.then_inc(z_ready, 1)

            def r(b):
                after(act, r_done, b)
                after(act, l3_done, b - 1)
                act.activation(rr[:, :], ps_h[0:K, 0:S], ACT.Identity, bias=pb[0:K, PB_ULAST:PB_ULAST + 1]).then_inc(rr_ready, 1)

            def step(i, j):
                if has(i + 1):
                    least_scores(i + 1)
                if has(i - 1):
                    z(i - 1)
                if has(i + 3):
                    y(i + 3)
                if has(i + 1):
                    exp(i + 1)
                if has(i + 4):
                    make_w1(i + 4)
                if has(i):
                    least_attended(i)
                if has(i - 1):
                    r(i - 1)
                if has(i):
                    make_wo(i)
                if has(i + 3):
                    take_keys(i + 3, (j + 1) % 2)
                more = has(i + 5) and (not isinstance(i, int) or i + 5 >= 2)
                if more:
                    load_bc(i + 5, (j + 1) % 2)
                if has(i + 4):
                    relu(i + 4)
                if has(i):
                    take_turned(i)
                if has(i - 1):
                    store(i - 1, (j + 1) % 2)
                if more:
                    load_x(i + 5, (j + 1) % 2)

            def early(i):
                if i == 0:
                    act.wait_ge(dec_out, 1)

            steps(act, step, early)
            for par in range(2):
                act.wait_ge(out_st[par], 16 * B // 2)

        @block.gpsimd
        def _(pool):
            pool.memset(bk[:, :], 0.0).then_inc(zero_k, 1)
            pool.memset(pick[:, :], 0.0).then_inc(pick_ready, 1)
            for n in range(PARTS):
                pool.wait_ge(pick_ready, n + 1)
                pool.memset(pick[32 * n:32 * n + 1, :], 1.0).then_inc(pick_ready, 1)
            pool.wait_ge(pick_ready, 1 + PARTS)

            def early(i):
                if i == -4:
                    pool.wait_ge(dec_done, 4)
                    pool.wait_ge(su_dve, SU_PARAMS)
                    pool.wait_ge(su_act, 2)
                    pool.wait_ge(rows_out, 16)
                    pool.memset(bv[:, :], 0.0).then_inc(zero_v, 1)

            def last_key_part(b, slot):
                parts = k3[:, slot, :, :]
                after(pool, k1_ready, b)
                pool.tensor_tensor(parts[:, 2, :], parts[:, 1, :], halves(parts[:, 1, :])[:, 1::2], ALU.subtract).then_inc(k3_ready, 1)

            def last_value_part(b, slot):
                after(pool, v1_ready, b)
                parts = v3[:, slot, :, :]
                pool.tensor_tensor(parts[:, 2, :], parts[:, 1, :], halves(parts[:, 1, :])[:, 1::2], ALU.subtract).then_inc(v3_ready, 1)

            def some_values_to_diagonal(b, slot):
                pool.wait_ge(zero_v, 1)
                after(pool, v3_ready, b)
                after(pool, av_done, b - 1)
                dst = bv[:, :].rearrange("p (w a t n) -> p w a t n", w=PARTS, a=2, t=G)
                src = v3[:, slot, :, :].rearrange("p w (v n) -> p w v n", v=2)
                for to, at, a, v in VALUE_BLOCKS[0:ON_POOL]:
                    pool.dma_start(dst[to:to + 16, :, a, to // 16, :], src[at:at + 16, :, v, :]).then_inc(bv_pool, 16)

            def make_x2(b, slot):
                after(pool, yc_ready, b)
                after(pool, x1_ready, b)
                after(pool, x3_ready, b - UNROLL)
                after(pool, key_done, b - UNROLL)
                pool.tensor_tensor(x2[:, slot, :], x1[:, :], yc[:, :], ALU.add).then_inc(x2_ready, 1)

            def probs(b):
                after(pool, inv_ready, b)
                after(pool, ex_ready, b)
                after(pool, a0_ready, b - 1)
                pool.tensor_tensor(pr[:, :].rearrange("p (u j) -> p u j", j=H), ex[:, :].rearrange("p (u j) -> p u j", j=H),
                                   sinv[:, :].unsqueeze(2).to_broadcast([P, NU, H]), ALU.mult).then_inc(pr_ready, 1)

            def make_x3(b, slot):
                after(pool, z_ready, b)
                after(pool, x2_ready, b)
                after(pool, r_done, b - 1)
                after(pool, xo_ready, b - 1)
                pool.tensor_tensor(x3[:, :], x2[:, slot, :], zz[:, :], ALU.add).then_inc(x3_ready, 1)

            def step(i, j):
                if has(i + 2):
                    last_key_part(i + 2, j % 2)
                if has(i + 1):
                    last_value_part(i + 1, (j + 1) % 2)
                if has(i - 1):
                    make_x3(i - 1, (j - 1) % UNROLL)
                if has(i + 3):
                    make_x2(i + 3, (j + 3) % UNROLL)
                if has(i + 1):
                    probs(i + 1)
                    some_values_to_diagonal(i + 1, (j + 1) % 2)

            steps(pool, step, early)

        @block.vector
        def _(dve):
            count = [0]

            def setup(ins):
                count[0] += 1
                ins.then_inc(su_dve, 1)
                dve.wait_ge(su_dve, count[0])

            dve.wait_ge(su_pe, 1)
            dve.wait_ge(ld_cond, 16 * 3)
            styles = ps_h[:, 0:3 * C * B].rearrange("p (n c b) -> p n c b", n=3, c=C)
            for n in range(3):
                for c in range(C):
                    ins = dve.tensor_scalar(sty[:, n, c, :], styles[:, n, c, :], GAIN if n == 0 else 1.0,
                                            afb[:, n, c:c + 1], ALU.mult, ALU.add)
                setup(ins)
            assert count[0] == SU_STY
            setup(dve.tensor_copy(pa_all[:, :, PA_STYLE1:PA_STYLE1 + 2].rearrange("p b c -> p c b"), sty[:, 0, :, :]))
            setup(dve.tensor_tensor(sty2[:, :, :, :].rearrange("p n c b -> p (n c b)"), sty[:, :, :, :].rearrange("p n c b -> p (n c b)"),
                                    sty[:, :, :, :].rearrange("p n c b -> p (n c b)"), ALU.mult))
            assert count[0] == SU_STY2
            dve.tensor_copy(pa_all[:, :, PA_STYLEK:PA_STYLEK + 2].rearrange("p b c -> p c b"), sty[:, 1, :, :])
            dve.tensor_copy(pb_all[:, :, PB_STYLEO:PB_STYLEO + 2].rearrange("p b c -> p c b"), sty[:, 2, :, :])
            dve.wait_ge(su_pe, 3)
            dve.tensor_scalar(rk0[:, :], ps_g[0:B, 0, 0:D], EPS, None, ALU.add)
            setup(dve.tensor_scalar(dem[:, :, :, :].rearrange("p n c b -> p (n c b)"), ps_k[:, 0:2 * C * B], EPS, None, ALU.add))
            assert count[0] == SU_VAR
            dve.wait_ge(su_act, 2)
            flat = [t[:, :, :, :].rearrange("p n c b -> p (n c b)") for t in (dem, dt1, dt2)]

            def newton(var, root, tmp, out):
                yield dve.reciprocal(tmp, root)
                yield dve.tensor_tensor(root, tmp, tmp, ALU.mult)
                yield dve.tensor_tensor(root, root, var, ALU.mult)
                yield dve.tensor_scalar(root, root, -0.5, 1.5, ALU.mult, ALU.add)
                yield dve.tensor_tensor(out, root, tmp, ALU.mult)

            rkd = rows[:, R_DK:R_DK + D]
            dve.tensor_copy(rows[:, 0:2 * HID], ps_f[0:B, 0:2 * HID])
            dve.tensor_copy(rows[:, R_UG:R_UG + 2 * D], ps_1[0:B, :])
            for ins in newton(rk0[:, :], rk1[:, :], kx[0:B, 0, 0:D], rkd):
                setup(ins)
            assert count[0] == SU_ROWS
            for ins in newton(flat[0], flat[1], flat[2], flat[0]):
                setup(ins)
            dve.tensor_copy(pa_all[:, :, PA_DEMOD1:PA_DEMOD1 + 2].rearrange("p b c -> p c b"), dem[:, 0, :, :])
            dve.tensor_copy(pb_all[:, :, PB_DEMODO:PB_DEMODO + 2].rearrange("p b c -> p c b"), dem[:, 1, :, :])
            setup(dve.memset(pb_all[:, :, PB_ULAST:PB_ULAST + 1], 0.0))
            dve.wait_ge(ld_small, 16 * N_SMALL)
            dve.wait_ge(su_pe, 4)
            setup(dve.tensor_scalar(pb_all[0:K, :, PB_ULAST], ps_k[0:K, 0:B], bdl[:, 0:1], None, ALU.add))
            assert count[0] == SU_PARAMS - 1
            low, least = kb3[32:64, :], kb3[64:96, :]
            setup(dve.tensor_tensor(least, least, halves(least)[:, 1::2], ALU.subtract))
            assert count[0] == SU_PARAMS
            dve.tensor_tensor(low, low, halves(low)[:, 1::2], ALU.subtract)
            dve.tensor_tensor(least, least, halves(least)[:, 1::2], ALU.subtract).then_inc(kb_ready, 1)

            def turn_decoder(part):
                dve.wait_ge(dec_done, part + 1)
                at = PB_U + part // 2 * K + part % 2 * (K // 2)
                dve.transpose(pb_all[:, :, at:at + K // 2].rearrange("p b k -> p k b"),
                              ps_g[:, part, 0:K // 2 * 32]).then_inc(dec_turned, 1)

            def decoder_bias():
                dve.wait_ge(dec_turned, 4)
                dst = pb_all[:, :, PB_U:PB_U + C * K]
                dve.tensor_tensor(dst, dst, bds[:, :, :].rearrange("p c k -> p (c k)").unsqueeze(1).to_broadcast([P, B, C * K]),
                                  ALU.add).then_inc(dec_out, 1)

            def early(i):
                if i == -4:
                    turn_decoder(0)
                    turn_decoder(1)
                if i == -3:
                    turn_decoder(2)
                    turn_decoder(3)
                    decoder_bias()

            both = [P, C, HID]

            def scale_weights(b, par):
                dve.wait_ge(bc_in[par], pair_count(b, par))
                row = bc[:, par, :]
                after(dve, down_done, b - 1)
                dve.tensor_tensor(wd[:, :, :], dpj[:, :, :], row[:, R_DG:R_DG + HID].unsqueeze(1).to_broadcast(both),
                                  ALU.mult).then_inc(wd_half, 1)
                after(dve, up_done, b - 1)
                dve.tensor_tensor(wu[:, :], upj[:, :], row[0:HID, R_UG:R_UG + D], ALU.mult).then_inc(wu_half, 1)

            def shift_weights(b, par):
                row = bc[:, par, :]
                after(dve, wd_half, b)
                dve.tensor_tensor(wd[:, :, :], wd[:, :, :], row[:, R_DB:R_DB + HID].unsqueeze(1).to_broadcast(both),
                                  ALU.add).then_inc(wd_ready, 1)
                after(dve, wu_half, b)
                dve.tensor_tensor(wu[:, :], wu[:, :], row[0:HID, R_UB:R_UB + D], ALU.add).then_inc(wu_ready, 1)

            def make_wk(b, par):
                after(dve, pa_ready, b)
                after(dve, key_done, b - 1)
                for c in range(C):
                    ins = dve.scalar_tensor_tensor(out=wk[:, c, :], in0=wks[:, c, :], scalar=pa[:, PA_STYLEK + c:PA_STYLEK + c + 1],
                                                   in1=bc[:, par, R_DK:R_DK + D], op0=ALU.mult, op1=ALU.mult)
                ins.then_inc(wk_ready, 1)

            def make_x1(b, par):
                after(dve, up_done, b)
                after(dve, l1_done, b - 1)
                after(dve, x2_ready, b - 1)
                dve.scalar_tensor_tensor(out=x1[:, :], in0=xin[:, par, :], scalar=2.0, in1=ps_f[:, :],
                                         op0=ALU.mult, op1=ALU.add).then_inc(x1_ready, 1)

            def clip(b):
                after(dve, y1_ready, b)
                after(dve, x2_ready, b - 1)
                dve.tensor_scalar(yc[:, :], y1[:, :], -CLAMP, CLAMP, ALU.max, ALU.min).then_inc(yc_ready, 1)

            def turn_keys(b, slot):
                after(dve, kx_ready, b)
                after(dve, s_done, b - 2)
                dve.transpose(k3[:, slot, 0, :], kx[:, slot, :].rearrange("p (a h d) -> p h a d", a=2, h=H)).then_inc(k0_ready, 1)

            def middle_key_part(b, slot):
                parts = k3[:, slot, :, :]
                after(dve, k0_ready, b)
                dve.tensor_tensor(parts[:, 1, :], parts[:, 0, :], halves(parts[:, 0, :])[:, 1::2], ALU.subtract).then_inc(k1_ready, 1)

            def turn_values(b, slot):
                after(dve, kx_ready, b)
                after(dve, bv_in, b - 2, 16 * (16 - ON_POOL))
                after(dve, bv_pool, b - 2, 16 * ON_POOL)
                dve.transpose(v3[:, slot, 0, :].rearrange("p (v d g) -> p d v g", v=2, d=DH),
                              kx[:, slot, :].rearrange("p (a j d) -> p d a j", a=2, j=H)).then_inc(v0_ready, 1)

            def middle_value_part(b, slot):
                after(dve, v0_ready, b)
                parts = v3[:, slot, :, :]
                dve.tensor_tensor(parts[:, 1, :], parts[:, 0, :], halves(parts[:, 0, :])[:, 1::2], ALU.subtract).then_inc(v1_ready, 1)

            def by_group(t):
                return t[:, :].rearrange("p (b u h) -> p b u h", b=NU // PER_BANK, u=PER_BANK)

            def middle_scores(b):
                after(dve, slo_ready, b)
                dve.tensor_tensor(by_group(sc), magnitude[:, 1], by_group(sc), ALU.add).then_inc(smid_ready, 1)

            def greatest_scores(b):
                after(dve, smid_ready, b)
                dve.tensor_tensor(by_group(sc), magnitude[:, 0], by_group(sc), ALU.add).then_inc(sc_ready, 1)

            def middle_attended(b):
                after(dve, alo_ready, b)
                dve.tensor_tensor(by_group(av), magnitude[:, 1], by_group(av), ALU.add).then_inc(amid_ready, 1)

            def greatest_attended(b):
                after(dve, amid_ready, b)
                dve.tensor_tensor(by_group(av), magnitude[:, 0], by_group(av), ALU.add).then_inc(av_ready, 1)

            def softmax_shift(b):
                after(dve, sc_ready, b)
                scores = sc[:, :].rearrange("p (u j) -> p u j", j=H)
                dve.tensor_reduce(smax[:, :], scores, AX.X, ALU.max).then_inc(max_ready, 1)
                after(dve, max_ready, b)
                dve.tensor_tensor(scores, scores, smax[:, :].unsqueeze(2).to_broadcast([P, NU, H]), ALU.subtract).then_inc(sd_ready, 1)

            def softmax_sum(b):
                after(dve, ex_ready, b)
                dve.tensor_reduce(ssum[:, :], ex[:, :].rearrange("p (u j) -> p u j", j=H), AX.X, ALU.add).then_inc(sum_ready, 1)

            def softmax_inverse(b):
                after(dve, sum_ready, b)
                after(dve, pr_ready, b - 1)
                dve.reciprocal(sinv[:, :], ssum[:, :]).then_inc(inv_ready, 1)

            def turn_probs(b):
                after(dve, pr_ready, b)
                after(dve, av_done, b - 1)
                dve.transpose(a3[:, 0, :], pr[:, :].rearrange("p (v g j) -> p g v j", v=2, j=H)).then_inc(a0_ready, 1)

            def middle_prob_part(b):
                after(dve, a0_ready, b)
                dve.tensor_tensor(a3[:, 1, :], a3[:, 0, :], halves(a3[:, 0, :])[:, 1::2], ALU.subtract).then_inc(a1_ready, 1)

            def last_prob_part(b):
                after(dve, a1_ready, b)
                dve.tensor_tensor(a3[:, 2, :], a3[:, 1, :], halves(a3[:, 1, :])[:, 1::2], ALU.subtract).then_inc(a3_ready, 1)

            def turn_attended(b):
                after(dve, av_ready, b)
                after(dve, t_done, b - 1)
                dve.transpose(on[:, :].rearrange("p (v h d) -> p h v d", v=2, h=H),
                              av[:, :].rearrange("p (g a h) -> p h a g", a=2, h=H)).then_inc(on_ready, 1)

            def make_out(b, par):
                after(dve, l3_done, b)
                after(dve, x3_ready, b)
                if not isinstance(b, int) or b >= 2:
                    dve.wait_ge(out_st[par], (b - par) * 8)
                dve.tensor_tensor(xo[:, par, :], x3[:, :], ps_f[:, :], ALU.add).then_inc(xo_ready, 1)

            def step(i, j):
                if has(i + 3):
                    make_wk(i + 3, (j + 1) % 2)
                if has(i + 1):
                    middle_scores(i + 1)
                if has(i + 3):
                    make_x1(i + 3, (j + 1) % 2)
                if has(i + 1):
                    greatest_scores(i + 1)
                if has(i + 4):
                    scale_weights(i + 4, j % 2)
                if has(i + 1):
                    softmax_shift(i + 1)
                if has(i + 4):
                    shift_weights(i + 4, j % 2)
                if has(i + 3):
                    clip(i + 3)
                if has(i + 1):
                    softmax_sum(i + 1)
                if has(i + 2):
                    turn_values(i + 2, j % 2)
                if has(i + 1):
                    softmax_inverse(i + 1)
                if has(i):
                    middle_attended(i)
                if has(i + 2):
                    middle_value_part(i + 2, j % 2)
                if has(i):
                    greatest_attended(i)
                    turn_attended(i)
                if has(i + 3):
                    turn_keys(i + 3, (j + 1) % 2)
                if has(i - 1):
                    make_out(i - 1, (j + 1) % 2)
                if has(i + 3):
                    middle_key_part(i + 3, (j + 1) % 2)
                if has(i + 1):
                    turn_probs(i + 1)
                    middle_prob_part(i + 1)
                    last_prob_part(i + 1)

            steps(dve, step, early)


def kernel(x, cond_512, L0_cond_down_project, L0_cond_down_gamma, L0_cond_down_beta, L0_cond_up_project,
           L0_cond_up_gamma, L0_cond_up_beta, L1_cond_weight, L1_cond_bias, L1_cond_affine_w, L1_cond_affine_b,
           L2_cond_k_aff_w, L2_cond_k_aff_b, L2_cond_k_w, L2_cond_k_b, L2_cond_o_aff_w, L2_cond_o_aff_b,
           L2_cond_o_w, L2_cond_o_b, L3_cond_W_dec, L3_cond_b_dec, L3_cond_V):
    import numpy as _np
    import concourse.bacc as _bacc
    from concourse import mybir as _mybir
    from concourse.bass_utils import run_bass_kernel_spmd as _run

    B, S, D = x.shape
    K = L3_cond_V.shape[0]

    def chunks(w):
        w = _np.asarray(w)
        return w.reshape(D // 128, 128, -1).transpose(1, 0, 2)

    def column(v):
        return _np.asarray(v).reshape(D // 128, 128).T

    arrays = {
        "xT": _np.asarray(x).transpose(0, 2, 1).reshape(B, D // 128, 128, S).transpose(0, 2, 1, 3),
        "condT": _np.asarray(cond_512).T,
        "from_cond": _np.concatenate([_np.asarray(L1_cond_affine_w).T, _np.asarray(L2_cond_k_aff_w).T,
                                      _np.asarray(L2_cond_o_aff_w).T, _np.asarray(L0_cond_down_gamma),
                                      _np.asarray(L0_cond_down_beta), _np.asarray(L0_cond_up_gamma),
                                      _np.asarray(L0_cond_up_beta)], 1),
        "w3T": _np.stack([chunks(_np.asarray(w).T) for w in (L1_cond_weight, L2_cond_k_w, L2_cond_o_w)], 1),
        "columns": _np.stack([column(v) for v in (L1_cond_affine_b, L2_cond_k_aff_b, L2_cond_o_aff_b,
                                                  L1_cond_bias, L2_cond_o_b)], 1),
        "dproj": chunks(L0_cond_down_project),
        "uproj": _np.asarray(L0_cond_up_project),
        "kb": _np.asarray(L2_cond_k_b).reshape(1, D),
        "wdec": _np.asarray(L3_cond_W_dec),
        "bdec": chunks(_np.asarray(L3_cond_b_dec)[:D * K].reshape(D, K)),
        "bdec_last": _np.asarray(L3_cond_b_dec)[D * K:].reshape(K, 1),
        "vmat": _np.asarray(L3_cond_V),
        "ident": _np.eye(128, dtype=_np.float32),
    }
    arrays = {n: _np.ascontiguousarray(a) for n, a in arrays.items()}
    nc = _bacc.Bacc("TRN2", target_bir_lowering=False, num_devices=1)
    args = [nc.dram_tensor(n, a.shape, _mybir.dt.from_np(a.dtype), kind="ExternalInput").ap() for n, a in arrays.items()]
    args.append(nc.dram_tensor("outT", arrays["xT"].shape, _mybir.dt.float32, kind="ExternalOutput").ap())
    build(nc, *args)
    r = _run(nc, [arrays], core_ids=[0])
    out = _np.asarray(r.results[0]["outT"])
    return out.transpose(0, 2, 1, 3).reshape(B, D, S).transpose(0, 2, 1)
```
